# Optimizing a Trainium2 kernel written in Bass

```python
import numpy as np
import jax
import jax.numpy as jnp

def _softmax(x, axis=-1):
    return jax.nn.softmax(x, axis=axis)

def _gelu(x):
    return jax.nn.gelu(x, approximate=True)

def _silu(x):
    return jax.nn.silu(x)

def _sigmoid(x):
    return jax.nn.sigmoid(x)

def _layernorm(x, axis=-1, eps=1e-05):
    m = jnp.mean(x, axis=axis, keepdims=True)
    v = jnp.var(x, axis=axis, keepdims=True)
    return (x - m) / jnp.sqrt(v + eps)

def _scatter_add(tgt, idx, src, axis=0):
    return tgt.at[idx].add(src)

def _segment_sum(src, seg, n):
    return jax.ops.segment_sum(src, seg, n)
kernel_name = 'mk_xattn_seq_d1_seqx_r4_dbc7b7'

def setup_inputs(seed: int=0):
    np.random.seed(seed)
    _w = jnp.asarray

    def _rec_inputs():
        import jax
        import jax.numpy as jnp
        _rk = jax.random.key(seed)
        x = -0.0001233 + 1 * jax.random.normal(jax.random.fold_in(_rk, 1), (16, 128, 320), jnp.float32)
        _lenS = 128 - jax.random.randint(jax.random.fold_in(_rk, 7), (16,), 0, max(1, 128 // 4) + 1, jnp.int32)
        _lenS2 = 128 - jax.random.randint(jax.random.fold_in(_rk, 8), (16,), 0, max(1, 128 // 4) + 1, jnp.int32)
        _ctx_2048P = jax.random.normal(jax.random.fold_in(_rk, 11), (16, 16, 512), jnp.float32)
        _ctx_2048c = jax.random.dirichlet(jax.random.fold_in(_rk, 511), 0.3 * jnp.ones((16,), jnp.float32), (16, 128))
        _ctx_2048t = jnp.einsum('bsk,bkd->bsd', _ctx_2048c, _ctx_2048P)
        _ctx_2048t = _ctx_2048t * jax.lax.rsqrt(jnp.mean(jnp.square(_ctx_2048t)) + 1e-12) * 0.953939
        ctx_2048 = 0.00266749 + 0.998873 * (_ctx_2048t + 0.3 * jax.random.normal(jax.random.fold_in(_rk, 611), (16, 128, 512), jnp.float32))
        return (x, ctx_2048)
    x, ctx_2048 = _rec_inputs()

    def _L0_xattn_setup():
        import jax, jax.numpy as jnp
        import numpy as np
        B, S, C = (2, 1024, 320)
        CA = 512
        HEADS = 20
        HD = C // HEADS
        N_TXT, N_OBJ, N_OTH, N_IP = (77, 4, 4, 16)
        SCALE_OBJ = SCALE_OTH = SCALE_IP = 1.0
        RESCALE = 1.0

        def _heads(x):
            b, l, _ = x.shape
            return x.reshape(b, l, HEADS, HD).transpose(0, 2, 1, 3)

        def _merge(x):
            b, h, l, d = x.shape
            return x.transpose(0, 2, 1, 3).reshape(b, l, h * d)

        def _sdpa(q, k, v):
            scale = 1.0 / np.sqrt(HD).astype(np.float32)
            s = jnp.einsum('bhqd,bhkd->bhqk', q, k) * scale
            p = jax.nn.softmax(s, axis=-1)
            return jnp.einsum('bhqk,bhkd->bhqd', p, v)
        key = jax.random.key(seed)
        ks = jax.random.split(key, 16)
        g = lambda k, shp, fan: jax.random.normal(k, shp, jnp.float32) / np.sqrt(fan).astype(np.float32)
        return {'hidden_states': jax.random.normal(ks[0], (B, S, C), jnp.float32), 'encoder_hidden_states': jax.random.normal(ks[1], (B, N_TXT + N_OBJ + N_OTH + N_IP, CA), jnp.float32), 'to_q_w': g(ks[2], (C, C), C), 'to_k_w': g(ks[3], (CA, C), CA), 'to_v_w': g(ks[4], (CA, C), CA), 'to_k_object_w': g(ks[5], (CA, C), CA), 'to_v_object_w': g(ks[6], (CA, C), CA), 'to_k_others_w': g(ks[7], (CA, C), CA), 'to_v_others_w': g(ks[8], (CA, C), CA), 'to_k_ip_w': g(ks[9], (CA, C), CA), 'to_v_ip_w': g(ks[10], (CA, C), CA), 'to_out_w': g(ks[11], (C, C), C), 'to_out_b': jnp.zeros((C,), jnp.float32)}
    _L0_xattn_all = _L0_xattn_setup()
    _L0_xattn_in = {k: v for k, v in _L0_xattn_all.items() if k in ('to_q_w', 'to_k_w', 'to_v_w', 'to_k_object_w', 'to_v_object_w', 'to_k_others_w', 'to_v_others_w', 'to_k_ip_w', 'to_v_ip_w', 'to_out_w', 'to_out_b')}
    del _L0_xattn_all
    return {'x': x, 'ctx_2048': ctx_2048, 'L0_xattn_to_q_w': _L0_xattn_in['to_q_w'], 'L0_xattn_to_k_w': _L0_xattn_in['to_k_w'], 'L0_xattn_to_v_w': _L0_xattn_in['to_v_w'], 'L0_xattn_to_k_object_w': _L0_xattn_in['to_k_object_w'], 'L0_xattn_to_v_object_w': _L0_xattn_in['to_v_object_w'], 'L0_xattn_to_k_others_w': _L0_xattn_in['to_k_others_w'], 'L0_xattn_to_v_others_w': _L0_xattn_in['to_v_others_w'], 'L0_xattn_to_k_ip_w': _L0_xattn_in['to_k_ip_w'], 'L0_xattn_to_v_ip_w': _L0_xattn_in['to_v_ip_w'], 'L0_xattn_to_out_w': _L0_xattn_in['to_out_w'], 'L0_xattn_to_out_b': _L0_xattn_in['to_out_b']}

def reference(x, ctx_2048, L0_xattn_to_q_w, L0_xattn_to_k_w, L0_xattn_to_v_w, L0_xattn_to_k_object_w, L0_xattn_to_v_object_w, L0_xattn_to_k_others_w, L0_xattn_to_v_others_w, L0_xattn_to_k_ip_w, L0_xattn_to_v_ip_w, L0_xattn_to_out_w, L0_xattn_to_out_b):
    import jax
    import jax.numpy as jnp

    def _L0_xattn_ref(hidden_states, encoder_hidden_states, to_q_w, to_k_w, to_v_w, to_k_object_w, to_v_object_w, to_k_others_w, to_v_others_w, to_k_ip_w, to_v_ip_w, to_out_w, to_out_b):
        import jax, jax.numpy as jnp
        import numpy as np
        B, S, C = (2, 1024, 320)
        CA = 512
        HEADS = 20
        HD = C // HEADS
        N_TXT, N_OBJ, N_OTH, N_IP = (77, 4, 4, 16)
        SCALE_OBJ = SCALE_OTH = SCALE_IP = 1.0
        RESCALE = 1.0

        def _heads(x):
            b, l, _ = x.shape
            return x.reshape(b, l, HEADS, HD).transpose(0, 2, 1, 3)

        def _merge(x):
            b, h, l, d = x.shape
            return x.transpose(0, 2, 1, 3).reshape(b, l, h * d)

        def _sdpa(q, k, v):
            scale = 1.0 / np.sqrt(HD).astype(np.float32)
            s = jnp.einsum('bhqd,bhkd->bhqk', q, k) * scale
            p = jax.nn.softmax(s, axis=-1)
            return jnp.einsum('bhqk,bhkd->bhqd', p, v)
        residual = hidden_states
        end = N_TXT
        ehs_txt = encoder_hidden_states[:, :end]
        ehs_obj = encoder_hidden_states[:, end:end + N_OBJ]
        ehs_oth = encoder_hidden_states[:, end + N_OBJ:end + N_OBJ + N_OTH]
        ehs_ip = encoder_hidden_states[:, end + N_OBJ + N_OTH:]
        q = _heads(hidden_states @ to_q_w)
        h_txt = _sdpa(q, _heads(ehs_txt @ to_k_w), _heads(ehs_txt @ to_v_w))
        h_obj = _sdpa(q, _heads(ehs_obj @ to_k_object_w), _heads(ehs_obj @ to_v_object_w))
        h_oth = _sdpa(q, _heads(ehs_oth @ to_k_others_w), _heads(ehs_oth @ to_v_others_w))
        h_ip = _sdpa(q, _heads(ehs_ip @ to_k_ip_w), _heads(ehs_ip @ to_v_ip_w))
        out = _merge(h_txt) + SCALE_OBJ * _merge(h_obj) + SCALE_OTH * _merge(h_oth) + SCALE_IP * _merge(h_ip)
        out = out @ to_out_w + to_out_b
        out = (out + residual) / RESCALE
        return out
    x = _L0_xattn_ref(x, ctx_2048, L0_xattn_to_q_w, L0_xattn_to_k_w, L0_xattn_to_v_w, L0_xattn_to_k_object_w, L0_xattn_to_v_object_w, L0_xattn_to_k_others_w, L0_xattn_to_v_others_w, L0_xattn_to_k_ip_w, L0_xattn_to_v_ip_w, L0_xattn_to_out_w, L0_xattn_to_out_b)
    return x

_drawn_inputs = setup_inputs


def setup_inputs(seed=0):
    import zlib

    import numpy as np

    out = dict(_drawn_inputs(seed))
    spreads = {'L0_xattn_to_out_b': (0.0, 0.1)}
    factors = {}
    for name, (base, spread) in spreads.items():
        noise = np.random.default_rng([zlib.crc32(name.encode()), seed]).standard_normal(out[name].shape)
        drawn = base * np.exp(spread * noise) if base else spread * noise
        out[name] = jnp.asarray(drawn.astype(out[name].dtype))
    for name, factor in factors.items():
        out[name] = (out[name] * factor).astype(out[name].dtype)
    return out
```

```python
from contextlib import ExitStack

import numpy as np

import concourse.bass as bass
from concourse import mybir

F32 = mybir.dt.float32
BF16 = mybir.dt.bfloat16
ALU = mybir.AluOpType
ACT = mybir.ActivationFunctionType
AX_X = mybir.AxisListType.X

B, S, C, CA = 16, 128, 320, 512
H, HD = 20, 16
G = 4
N_TXT, N_OBJ, N_OTH = 77, 4, 4
N_IP = S - N_TXT - N_OBJ - N_OTH
N_BIG = N_TXT + N_IP
N_SML = N_OBJ
PAIRS = B // 2
T2 = 2 * S
SCALE = 1.0 / float(np.sqrt(HD))
KC = CA // 128
XC = [128, 128, C - 256]
HT = 4
NT = H // HT
SLOTS_Q = [0, 0, 0, 1, 1, 2]
SLOTS_K = [0, 1, 2, 0, 1, 0]
KS = 16 * len(SLOTS_Q)
HH = H // 2
MR = 3 * HH * G
VB = (G + 1) * C
OW = (G + 1) * HD
RELAY = 12 * 16
N_VDMA = 4 * 16


class Pair:

    def __init__(self, index, parity, use):
        self.i, self.par, self.use = index, parity, use


def pair(i):
    return Pair(i, i % 2, i // 2)


def build(nc, xT, xn, cM, cS, wq, wkt, wvt, wki, wvi, wko, wvo, wkh, wvh, wo, bo, ident_d, sel_d, spread_d, out):
    ctx = ExitStack()
    with ctx:
        def sb(name, shape, dt=F32):
            return ctx.enter_context(nc.sbuf_tensor(name, shape, dt))

        def ps(name, shape):
            return ctx.enter_context(nc.psum_tensor(name, shape, F32))

        def sem(name):
            return ctx.enter_context(nc.semaphore(name))

        wq_sb = sb("wq_sb", [128, 3, C])
        wo_sb = sb("wo_sb", [128, 3, C])
        wk_sb = [sb(f"wk_sb{g}", [128, KC, C]) for g in range(2)]
        wv_sb = [sb(f"wv_sb{g}", [128, KC, C]) for g in range(2)]
        wks_sb = sb("wks_sb", [128, 2, KC, C])
        wvs_sb = sb("wvs_sb", [128, 2, KC, C])
        bias = sb("bias", [128, C])
        ident = sb("ident", [128, 128])
        identb = sb("identb", [128, 128], BF16)
        sel_f = sb("sel_f", [MR, HH * 128])
        sel = sb("sel", [MR, HH, 128], BF16)
        xT_sb = sb("xT_sb", [128, 2, 3, T2])
        cT_sb = sb("cT_sb", [128, 2, KC, 2 * N_BIG])
        cS_sb = sb("cS_sb", [128, KC, 2 * B * N_SML])
        xn_sb = sb("xn_sb", [128, 2, C])
        xb = sb("xb", [128, 2, C])
        qp = sb("qp", [128, 3, 3, T2], BF16)
        kp = sb("kp", [128, 3, 3, 2, S], BF16)
        ksm = sb("ksm", [128, 3, 3, B, 2 * N_SML], BF16)
        ksr = sb("ksr", [128, 3, B, 2 * N_SML])
        qr = sb("qr", [128, 3, T2])
        kr = sb("kr", [128, 3, 2, N_BIG])
        qst = [sb(f"qst{p}", [KS, H, T2], BF16) for p in range(2)]
        kst = [sb(f"kst{p}", [KS, H, T2], BF16) for p in range(2)]
        vbd = sb("vbd", [128, 2, 2, G + 1, C])
        vip = sb("vip", [2 * N_IP, C])
        vsm = sb("vsm", [B * N_SML, 2, C])
        vs_dram = nc.dram_tensor("vs_dram", (PAIRS, 2, 2 * N_SML, C), F32, kind="Internal").ap()
        nm = sb("nm", [128, H, G])
        nmr = sb("nmr", [128, 2, HH * G])
        nmr2 = sb("nmr2", [128, 2, HH * G])
        mp = sb("mp", [128, 2, 3, HH * G], BF16)
        mT = sb("mT", [MR, 2, 128], BF16)
        pT = sb("pT", [128, NT, HT, S])
        rz = sb("rz", [128, 2, HT, G])
        og = sb("og", [128, 2, H, G, HD])
        os = sb("os", [128, H, 2, HD])
        on = sb("on", [128, 2, H * HD])
        oT = sb("oT", [128, 2, 3, 128])
        res = sb("res", [128, 2, C])

        ps_s = [ps(f"ps_s{k}", [128, HT, S]) for k in range(2)]
        ps_t = [ps(f"ps_t{k}", [128, HT, S]) for k in range(2)]
        ps_o = [ps(f"ps_o{k}", [128, 512]) for k in range(2)]
        ps_p = [ps(f"ps_p{k}", [128, 512]) for k in range(2)]

        w_small, w_q, w_k, w_v, w_o = (sem(n) for n in ("w_small", "w_q", "w_k", "w_v", "w_o"))
        consts, spread_in = sem("consts"), sem("spread_in")
        x_in = [sem(f"x_in{p}") for p in range(2)]
        c_in = [sem(f"c_in{p}") for p in range(2)]
        xn_in = [sem(f"xn_in{b}") for b in range(2)]
        casts = sem("casts")
        q_done, k_done, v_done = sem("q_done"), sem("k_done"), sem("v_done")
        q_hi, k_hi, q_rest, k_rest = sem("q_hi"), sem("k_hi"), sem("q_rest"), sem("k_rest")
        q_mid, k_mid, k_small = sem("q_mid"), sem("k_mid"), sem("k_small")
        q_parts, k_parts = sem("q_parts"), sem("k_parts")
        q_st = [sem(f"q_st{p}") for p in range(2)]
        k_st = [sem(f"k_st{p}") for p in range(2)]
        v_put, vip_out = sem("v_put"), sem("vip_out")
        v_in = [sem(f"v_in{p}") for p in range(2)]
        s_done, s_max, m_chain, m_parts = sem("s_done"), sem("s_max"), sem("m_chain"), sem("m_parts")
        mt_done, mt_out = sem("mt_done"), sem("mt_out")
        t_done, t_exp, pv_done = sem("t_done"), sem("t_exp"), sem("pv_done")
        z_inv, o_norm, o_half, o_sum = sem("z_inv"), sem("o_norm"), sem("o_half"), sem("o_sum")
        ot_done, ot_out, out_done, xb_done, res_done = (
            sem(n) for n in ("ot_done", "ot_out", "out_done", "xb_done", "res_done"))
        stored = [sem(f"stored{b}") for b in range(2)]
        sm_k, sm_v, sm_hi, sm_rest, sm_mid, sm_parts, sm_vout, sm_dram = (
            sem(n) for n in ("sm_k", "sm_v", "sm_hi", "sm_rest", "sm_mid", "sm_parts", "sm_vout", "sm_dram"))

        block = ctx.enter_context(nc.Block())

        @block.sync
        def _(sp):
            xn_v = xn.rearrange("(p b q) n -> p b q n", b=2, q=S)
            out_v = out.rearrange("(p b q) n -> p b q n", b=2, q=S)

            def addresses(i, *tensors):
                if not isinstance(i, int):
                    for t in tensors:
                        sp.snap(i * (t.size() // t.shape[0]) * 4)

            def load_tokens(i, p):
                sp.dma_start(xT_sb[:, p, 0:2, :], xT[i, 0:256, :].rearrange("(k p) t -> p k t", p=128)).then_inc(x_in[p], 16)
                sp.dma_start(xT_sb[0:XC[2], p, 2, :], xT[i, 256:C, :]).then_inc(x_in[p], 16)
                sp.dma_start(cT_sb[:, p, :, :], cM[i].rearrange("(k p) t -> p k t", p=128)).then_inc(c_in[p], 16)

            def load_next(q):
                addresses(q.i, xT, cM)
                sp.wait_ge(v_done, 3 * (q.i - 1))
                load_tokens(q.i, q.par)

            def stack(q, parts, slots, to, done):
                for n, part in enumerate(slots):
                    rows = slice(16 * n, 16 * n + 16)
                    sp.dma_start(to[q.par][rows, 0:16, :], parts[:, part, 0:2, :]).then_inc(done[q.par], 16)
                    sp.dma_start(to[q.par][rows, 16:H, :], parts[0:XC[2], part, 2, :]).then_inc(done[q.par], 16)

            kp_v = kp[:, :, :, :, :].rearrange("p a c b t -> p a c (b t)")

            def stack_q(q):
                sp.wait_ge(q_parts, 2 * (q.i + 1))
                stack(q, qp, SLOTS_Q, qst, q_st)

            def stack_k(q):
                sp.wait_ge(k_small, q.i + 1)
                sp.wait_ge(k_parts, 2 * (q.i + 1))
                stack(q, kp_v, SLOTS_K, kst, k_st)

            def spread_v(q):
                for g in range(2):
                    k0 = N_BIG + g * N_SML
                    sp.dma_start(vbd[k0:k0 + N_SML, q.par, :, 2 + g, :],
                                 vs_dram[q.i, :, g * N_SML:(g + 1) * N_SML, :].rearrange("b t n -> t b n"))\
                      .then_inc(v_in[q.par], 16)
                sp.wait_ge(vip_out, q.i + 1)
                for b in range(2):
                    sp.dma_start(vbd[N_TXT:N_BIG, q.par, b, 1, :], vip[b * N_IP:(b + 1) * N_IP, :])\
                      .then_inc(v_in[q.par], 16)

            def load_x(a, b):
                sp.dma_start(xn_sb[:, b, :], xn_v[a, b]).then_inc(xn_in[b], 16)

            def store(a, b):
                sp.wait_ge(res_done, 2 * a + b + 1)
                sp.dma_start(out_v[a, b], res[:, b, :]).then_inc(stored[b], 16)

            def step(q, a, first=False):
                if a is not None:
                    if not first:
                        sp.wait_ge(xb_done, 2 * a - 1)
                    load_x(a, 0)
                if q is not None:
                    stack_q(q)
                if a is not None and not first:
                    store(a - 1, 1)
                    sp.wait_ge(xb_done, 2 * a)
                    load_x(a, 1)
                elif first:
                    load_x(a, 1)
                if q is not None:
                    stack_k(q)
                if a is not None:
                    store(a, 0)
                if q is not None:
                    if q.par is not None and not (isinstance(q.i, int) and q.i < 2):
                        sp.wait_ge(pv_done, 2 * NT * (q.i - 1))
                    spread_v(q)

            sp.dma_start(cS_sb[:, :, :], cS.rearrange("(k p) t -> p k t", p=128)).then_inc(w_small, 16)
            for g, (wk, wv) in enumerate(((wko, wvo), (wkh, wvh))):
                sp.dma_start(wks_sb[:, g, :, :], wk.rearrange("(k p) n -> p k n", p=128)).then_inc(w_small, 16)
                sp.dma_start(wvs_sb[:, g, :, :], wv.rearrange("(k p) n -> p k n", p=128)).then_inc(w_small, 16)
            sp.dma_start(wq_sb[:, 0:2, :], wq[0:256, :].rearrange("(k p) n -> p k n", p=128)).then_inc(w_q, 16)
            sp.dma_start(wq_sb[0:XC[2], 2, :], wq[256:C, :]).then_inc(w_q, 16)
            load_tokens(0, 0)
            for g, wk in enumerate((wkt, wki)):
                sp.dma_start(wk_sb[g][:, :, :], wk.rearrange("(k p) n -> p k n", p=128)).then_inc(w_k, 16)
            for g, wv in enumerate((wvt, wvi)):
                sp.dma_start(wv_sb[g][:, :, :], wv.rearrange("(k p) n -> p k n", p=128)).then_inc(w_v, 16)
            sp.dma_start(ident[:, :], ident_d).then_inc(consts, 16)
            sp.dma_start(sel_f[:, :], sel_d).then_inc(consts, 16)
            sp.dma_start(bias[:, :], bo.partition_broadcast(128)).then_inc(consts, 16)
            for p in range(2):
                for b in range(2):
                    sp.dma_start(vbd[:, p, b, :, :], spread_d.rearrange("p (g n) -> p g n", g=G + 1)).then_inc(spread_in, 16)
            load_tokens(1, 1)
            sp.dma_start(wo_sb[:, 0:2, :], wo[0:256, :].rearrange("(k p) n -> p k n", p=128)).then_inc(w_o, 16)
            sp.dma_start(wo_sb[0:XC[2], 2, :], wo[256:C, :]).then_inc(w_o, 16)
            sp.wait_ge(sm_vout, 2)
            for g in range(2):
                sp.dma_start(vs_dram.rearrange("p b r n -> (p b) r n")[:, g * N_SML:(g + 1) * N_SML, :],
                             vsm[:, g, :]).then_inc(sm_dram, 16)
            sp.wait_ge(sm_dram, 32)
            sp.wait_ge(spread_in, 64)
            step(pair(0), None)
            load_next(pair(2))
            step(pair(1), 0, first=True)
            load_next(pair(3))
            step(pair(2), 1)
            with sp.Fori(0, (PAIRS - 4) // 2) as j:
                load_next(Pair(4 + 2 * j, 0, 2 + j))
                step(Pair(3 + 2 * j, 1, 1 + j), 2 + 2 * j)
                load_next(Pair(5 + 2 * j, 1, 2 + j))
                step(Pair(4 + 2 * j, 0, 2 + j), 3 + 2 * j)
            step(pair(PAIRS - 1), PAIRS - 2)
            step(None, PAIRS - 1)
            store(PAIRS - 1, 1)
            for b in range(2):
                sp.wait_ge(stored[b], 16 * PAIRS)

        @block.tensor
        def _(pe):
            def project_q01(q):
                pe.wait_ge(x_in[q.par], 32 * (q.use + 1))
                if not (isinstance(q.i, int) and q.i == 0):
                    pe.wait_ge(vip_out, q.i)
                for c in range(2):
                    for k in range(3):
                        mm = nc.tensor.matmul(ps_p[0][:, c * T2:(c + 1) * T2],
                                              wq_sb[0:XC[k], k, c * 128:(c + 1) * 128],
                                              xT_sb[0:XC[k], q.par, k, :], start=(k == 0), stop=(k == 2))
                mm.then_inc(q_done, 1)

            def project_q2(q):
                if not (isinstance(q.i, int) and q.i == 0):
                    pe.wait_ge(v_put, 2 * q.i)
                for k in range(3):
                    mm = nc.tensor.matmul(ps_p[1][0:XC[2], 0:T2], wq_sb[0:XC[k], k, 256:C],
                                          xT_sb[0:XC[k], q.par, k, :], start=(k == 0), stop=(k == 2))
                mm.then_inc(q_done, 1)

            def k_chunk(q, bank, at, c):
                w = XC[c]
                view = ps_p[bank][0:w, at:at + T2].rearrange("p (b t) -> p b t", b=2)
                for g, (t0, n) in enumerate(((0, N_TXT), (N_TXT, N_IP))):
                    rhs = cT_sb[:, q.par, :, 2 * t0:2 * (t0 + n)].rearrange("p k (b t) -> p k b t", b=2)
                    for k in range(KC):
                        mm = nc.tensor.matmul(view[:, :, t0:t0 + n], wk_sb[g][:, k, c * 128:c * 128 + w],
                                              rhs[:, k, :, :], start=(k == 0), stop=(k == KC - 1))
                return mm

            def project_k01(q):
                pe.wait_ge(c_in[q.par], 16 * (q.use + 1))
                pe.wait_ge(q_rest, 2 * q.i + 1)
                k_chunk(q, 0, 0, 0)
                k_chunk(q, 0, T2, 1).then_inc(k_done, 1)

            def project_k2(q):
                pe.wait_ge(q_rest, 2 * q.i + 2)
                k_chunk(q, 1, 0, 2).then_inc(k_done, 1)

            def project_v(q, n):
                if n < 2:
                    pe.wait_ge(k_rest, 2 * q.i + 1 + n)
                else:
                    pe.wait_ge(v_put, 2 * q.i + 1)
                t0, m = [(0, N_TXT), (N_TXT, N_TXT), (2 * N_TXT, 2 * N_IP)][n]
                for k in range(KC):
                    mm = nc.tensor.matmul(ps_p[n % 2][0:m, 0:C], cT_sb[:, q.par, k, t0:t0 + m],
                                          wv_sb[n // 2][:, k, :], start=(k == 0), stop=(k == KC - 1))
                mm.then_inc(v_done, 1)

            def score_tile(a, b, t, fresh):
                n = 2 * a.i + b
                if t >= 2:
                    pe.wait_ge(s_max, NT * n + t - 1)
                elif not fresh:
                    if t == 0:
                        pe.wait_ge(s_max, NT * n)
                    else:
                        pe.wait_ge(mt_out, n)
                for j in range(HT):
                    h = t * HT + j
                    mm = nc.tensor.matmul(ps_s[t % 2][:, j, :], qst[a.par][:, h, b * S:(b + 1) * S],
                                          kst[a.par][:, h, b * S:(b + 1) * S], start=True, stop=True)
                mm.then_inc(s_done, 1)

            def turn_maxima(a, b):
                n = 2 * a.i + b
                pe.wait_ge(m_parts, n + 1)
                for half in range(2):
                    mm = nc.tensor.matmul(ps_s[1][0:MR, half, :], mp[:, half, :, :].rearrange("p a m -> p (a m)"),
                                          identb[:, :], start=True, stop=True)
                mm.then_inc(mt_done, 1)

            def exp_tile(a, b, t, fresh):
                n = 2 * a.i + b
                bank = (b * (NT + 2) + 2 + t) % 2
                if t >= 2:
                    pe.wait_ge(t_exp, NT * n + t - 1)
                elif not fresh:
                    if t == 0:
                        pe.wait_ge(ot_out, n)
                    else:
                        pe.wait_ge(res_done, n)
                if t == 0:
                    pe.wait_ge(mt_out, n + 1)
                for j in range(HT):
                    h = t * HT + j
                    nc.tensor.matmul(ps_t[bank][:, j, :], kst[a.par][:, h, b * S:(b + 1) * S],
                                     qst[a.par][:, h, b * S:(b + 1) * S], start=True, stop=False)
                    mm = nc.tensor.matmul(ps_t[bank][:, j, :], sel[:, h % HH, :], mT[:, h // HH, :],
                                          start=False, stop=True)
                mm.then_inc(t_done, 1)

            def value_tile(a, b, t, fresh):
                n = 2 * a.i + b
                bank = (n0(b) + t) % 2
                if not (fresh and t < 2):
                    pe.wait_ge(o_norm, NT * n + t - 1)
                if t == 0:
                    pe.wait_ge(v_put, 2 * (a.i + 1))
                    pe.wait_ge(v_in[a.par], N_VDMA * (a.use + 1))
                pe.wait_ge(t_exp, NT * n + t + 1)
                for j in range(HT):
                    h = t * HT + j
                    mm = nc.tensor.matmul(ps_o[bank][:, j * OW:(j + 1) * OW], pT[:, t, j, :],
                                          vbd[:, a.par, b, :, h * HD:(h + 1) * HD], start=True, stop=True)
                mm.then_inc(pv_done, 1)

            def turn_heads(n, b_ring):
                pe.wait_ge(t_exp, NT * n - 1)
                pe.wait_ge(o_sum, n)
                bank = (b_ring * (NT + 2)) % 2
                b = 1 - b_ring
                flat = ps_t[bank][:, :, :].rearrange("p j t -> p (j t)")
                for c in range(3):
                    mm = nc.tensor.transpose(flat[0:XC[c], c * 128:(c + 1) * 128],
                                             on[:, b, c * 128:c * 128 + XC[c]], ident[:, :])
                mm.then_inc(ot_done, 1)

            def output(n, b_ring):
                pe.wait_ge(t_exp, NT * n)
                pe.wait_ge(ot_out, n)
                bank = (b_ring * (NT + 2) + 1) % 2
                flat = ps_t[bank][:, :, :].rearrange("p j t -> p (j t)")
                for c in range(3):
                    mm = nc.tensor.matmul(flat[:, 0:C], oT[0:XC[c], 1 - b_ring, c, :], wo_sb[0:XC[c], c, :],
                                          start=(c == 0), stop=(c == 2))
                mm.then_inc(out_done, 1)

            def step(q, a, first=False):
                for b in range(2):
                    fresh = first and b == 0
                    if a is not None:
                        n = 2 * a.i + b
                        if b == 0:
                            pe.wait_ge(q_st[a.par], RELAY * (a.use + 1))
                            pe.wait_ge(k_st[a.par], RELAY * (a.use + 1))
                        score_tile(a, b, 0, fresh)
                        score_tile(a, b, 1, fresh)
                    if q is not None:
                        project_q01(q) if b == 0 else project_v(q, 0)
                    if a is not None:
                        score_tile(a, b, 2, fresh)
                        score_tile(a, b, 3, fresh)
                        if not fresh:
                            turn_heads(n, b)
                    if q is not None:
                        project_q2(q) if b == 0 else project_v(q, 1)
                    if a is not None:
                        score_tile(a, b, 4, fresh)
                        if not fresh:
                            output(n, b)
                    if q is not None:
                        if b == 0:
                            project_k01(q)
                            project_k2(q)
                        else:
                            project_v(q, 2)
                    if a is not None:
                        turn_maxima(a, b)
                        for t in range(NT + 1):
                            if t < NT:
                                exp_tile(a, b, t, fresh)
                            if t >= 1:
                                value_tile(a, b, t - 1, fresh)

            pe.wait_ge(w_small, 80)
            pe.wait_ge(casts, 1)
            for g in range(2):
                for c in range(3):
                    w = XC[c]
                    view = ps_p[0][0:w, c * 128:(c + 1) * 128].rearrange("p (b r) -> p b r", b=B)
                    rhs = cS_sb[:, :, g * B * N_SML:(g + 1) * B * N_SML].rearrange("p k (b t) -> p k b t", b=B)
                    for k in range(KC):
                        mm = nc.tensor.matmul(view[:, :, g * N_SML:(g + 1) * N_SML],
                                              wks_sb[:, g, k, c * 128:c * 128 + w], rhs[:, k, :, :],
                                              start=(k == 0), stop=(k == KC - 1))
            mm.then_inc(sm_k, 1)
            for g in range(2):
                for k in range(KC):
                    mm = nc.tensor.matmul(ps_o[g][0:B * N_SML, 0:C], cS_sb[:, k, g * B * N_SML:(g + 1) * B * N_SML],
                                          wvs_sb[:, g, k, :], start=(k == 0), stop=(k == KC - 1))
                mm.then_inc(sm_v, 1)
            pe.wait_ge(sm_rest, 1)
            pe.wait_ge(w_q, 32)
            pe.wait_ge(w_k, 32)
            pe.wait_ge(w_v, 32)
            step(pair(0), None)
            pe.wait_ge(casts, 3)
            pe.wait_ge(spread_in, 64)
            pe.wait_ge(w_o, 32)
            pe.wait_ge(consts, 48)
            pe.wait_ge(sm_vout, 2)
            step(pair(1), pair(0), first=True)
            with pe.Fori(0, (PAIRS - 2) // 2) as j:
                step(Pair(2 + 2 * j, 0, 1 + j), Pair(1 + 2 * j, 1, j))
                step(Pair(3 + 2 * j, 1, 1 + j), Pair(2 + 2 * j, 0, 1 + j))
            step(None, pair(PAIRS - 1))
            turn_heads(B, 0)
            output(B, 0)

        @block.scalar
        def _(act):
            def q_high(q, c):
                act.wait_ge(q_done, 2 * q.i + 1 + c)
                if c == 0:
                    if not (isinstance(q.i, int) and q.i == 0):
                        act.wait_ge(q_st[1 - q.par], RELAY * (q.use + q.par))
                    nc.scalar.activation(qp[:, 0, 0:2, :].rearrange("p c t -> p (c t)"), ps_p[0][:, :],
                                         ACT.Copy).then_inc(q_hi, 1)
                else:
                    nc.scalar.activation(qp[0:XC[2], 0, 2, :], ps_p[1][0:XC[2], 0:T2], ACT.Copy).then_inc(q_hi, 1)

            def k_high(q, c):
                act.wait_ge(k_done, 2 * q.i + 1 + c)
                if c == 0:
                    if not (isinstance(q.i, int) and q.i == 0):
                        act.wait_ge(k_st[1 - q.par], RELAY * (q.use + q.par))
                    src = ps_p[0][:, :].rearrange("p (m t) -> p m t", t=S)
                    dst = kp[:, 0, 0:2, :, :].rearrange("p c b t -> p (c b) t")
                    nc.scalar.activation(dst[:, :, 0:N_BIG], src[:, :, 0:N_BIG], ACT.Copy).then_inc(k_hi, 1)
                    small = ksm[:, :, :, :, :].rearrange("p a c (i b) r -> p i (a c) b r", b=2)
                    nc.scalar.activation(kp[:, :, :, :, N_BIG:S].rearrange("p a c b r -> p (a c) b r"),
                                         small[:, q.i, :, :, :], ACT.Copy).then_inc(k_small, 1)
                else:
                    src = ps_p[1][0:XC[2], 0:T2].rearrange("p (m t) -> p m t", t=S)
                    nc.scalar.activation(kp[0:XC[2], 0, 2, :, 0:N_BIG], src[:, :, 0:N_BIG], ACT.Copy).then_inc(k_hi, 1)

            def q_middle(q):
                for c in range(2):
                    act.wait_ge(q_rest, 2 * q.i + 1 + c)
                    rows, cs = (128, slice(0, 2)) if c == 0 else (XC[2], slice(2, 3))
                    nc.scalar.activation(qp[0:rows, 1, cs, :], qr[0:rows, cs, :], ACT.Copy).then_inc(q_mid, 1)

            def k_middle(q):
                for c in range(2):
                    act.wait_ge(k_rest, 2 * q.i + 1 + c)
                    rows, cs = (128, slice(0, 2)) if c == 0 else (XC[2], slice(2, 3))
                    nc.scalar.activation(kp[0:rows, 1, cs, :, 0:N_BIG].rearrange("p c b t -> p (c b) t"),
                                         kr[0:rows, cs, :, :].rearrange("p c b t -> p (c b) t"), ACT.Copy).then_inc(k_mid, 1)

            def v_text(q, b):
                act.wait_ge(v_done, 3 * q.i + 1 + b)
                nc.scalar.activation(vbd[0:N_TXT, q.par, b, 0, :], ps_p[b][0:N_TXT, 0:C], ACT.Copy).then_inc(v_put, 1)

            def v_image(q):
                act.wait_ge(v_done, 3 * q.i + 3)
                if not (isinstance(q.i, int) and q.i == 0):
                    act.wait_ge(v_in[1 - q.par], N_VDMA * (q.use + q.par))
                nc.scalar.activation(vip[:, :], ps_p[0][0:2 * N_IP, 0:C], ACT.Copy).then_inc(vip_out, 1)

            def heads_out(n, b_ring):
                act.wait_ge(ot_done, n)
                bank = (b_ring * (NT + 2)) % 2
                flat = ps_t[bank][:, :, :].rearrange("p j t -> p (j t)")
                dst = oT[:, 1 - b_ring, :, :].rearrange("p c t -> p (c t)")
                nc.scalar.activation(dst[:, 0:256], flat[:, 0:256], ACT.Copy)
                nc.scalar.activation(dst[0:XC[2], 256:384], flat[0:XC[2], 256:384], ACT.Copy).then_inc(ot_out, 1)

            def maxima_out(a, b):
                n = 2 * a.i + b
                act.wait_ge(mt_done, n + 1)
                nc.scalar.activation(mT[:, :, :], ps_s[1][0:MR, 0:2, :], ACT.Copy).then_inc(mt_out, 1)

            def exponentials(a, b, t, fresh):
                n = 2 * a.i + b
                bank = (b * (NT + 2) + 2 + t) % 2
                act.wait_ge(t_done, NT * n + t + 1)
                if not fresh:
                    act.wait_ge(pv_done, NT * (n - 1) + t + 1)
                nc.scalar.activation(pT[:, t, :, :], ps_t[bank][:, :, :], ACT.Exp, scale=SCALE)\
                  .then_inc(t_exp, 1)

            def step(q, a, first=False):
                for b in range(2):
                    fresh = first and b == 0
                    if q is not None:
                        q_high(q, 0) if b == 0 else v_text(q, 0)
                    if a is not None and not fresh:
                        heads_out(2 * a.i + b, b)
                    if q is not None:
                        if b == 0:
                            q_high(q, 1)
                            q_middle(q)
                            k_high(q, 0)
                            k_high(q, 1)
                        else:
                            v_text(q, 1)
                            v_image(q)
                    if a is not None:
                        maxima_out(a, b)
                        for t in range(NT):
                            exponentials(a, b, t, fresh)
                            if t == 0 and b == 0 and q is not None:
                                k_middle(q)
                    elif b == 0:
                        k_middle(q)

            act.wait_ge(sm_k, 1)
            nc.scalar.activation(ksm[:, 0, :, :, :].rearrange("p c b r -> p (c b r)"), ps_p[0][:, 0:384],
                                 ACT.Copy).then_inc(sm_hi, 1)
            for g in range(2):
                act.wait_ge(sm_v, g + 1)
                nc.scalar.activation(vsm[:, g, :], ps_o[g][0:B * N_SML, 0:C], ACT.Copy).then_inc(sm_vout, 1)
            act.wait_ge(spread_in, 64)
            act.wait_ge(sm_parts, 1)
            step(pair(0), None)
            step(pair(1), pair(0), first=True)
            with act.Fori(0, (PAIRS - 2) // 2) as j:
                step(Pair(2 + 2 * j, 0, 1 + j), Pair(1 + 2 * j, 1, j))
                step(Pair(3 + 2 * j, 1, 1 + j), Pair(2 + 2 * j, 0, 1 + j))
            step(None, pair(PAIRS - 1))
            heads_out(B, 0)

        @block.vector
        def _(dve):
            def q_low(q, c):
                dve.wait_ge(q_hi, 2 * q.i + 1 + c)
                if not (isinstance(q.i, int) and q.i == 0):
                    dve.wait_ge(q_parts, 2 * q.i)
                if c == 0:
                    nc.vector.tensor_tensor(qr[:, 0:2, :].rearrange("p c t -> p (c t)"), ps_p[0][:, :],
                                            qp[:, 0, 0:2, :].rearrange("p c t -> p (c t)"), ALU.subtract).then_inc(q_rest, 1)
                else:
                    nc.vector.tensor_tensor(qr[0:XC[2], 2, :], ps_p[1][0:XC[2], 0:T2], qp[0:XC[2], 0, 2, :],
                                            ALU.subtract).then_inc(q_rest, 1)

            def k_low(q, c):
                dve.wait_ge(k_hi, 2 * q.i + 1 + c)
                if not (isinstance(q.i, int) and q.i == 0):
                    dve.wait_ge(k_parts, 2 * q.i)
                if c == 0:
                    src = ps_p[0][:, :].rearrange("p (m t) -> p m t", t=S)
                    hi = kp[:, 0, 0:2, :, :].rearrange("p c b t -> p (c b) t")
                    dst = kr[:, 0:2, :, :].rearrange("p c b t -> p (c b) t")
                    nc.vector.tensor_tensor(dst, src[:, :, 0:N_BIG], hi[:, :, 0:N_BIG], ALU.subtract).then_inc(k_rest, 1)
                else:
                    src = ps_p[1][0:XC[2], 0:T2].rearrange("p (m t) -> p m t", t=S)
                    nc.vector.tensor_tensor(kr[0:XC[2], 2, :, :], src[:, :, 0:N_BIG], kp[0:XC[2], 0, 2, :, 0:N_BIG],
                                            ALU.subtract).then_inc(k_rest, 1)

            def maxima(a, b, t, fresh):
                n = 2 * a.i + b
                dve.wait_ge(s_done, NT * n + t + 1)
                if t == 0 and not fresh:
                    dve.wait_ge(m_parts, n)
                src, hs = ps_s[t % 2], slice(t * HT, (t + 1) * HT)
                nc.vector.tensor_reduce(nm[:, hs, 0:1], src[:, :, 0:N_TXT], AX_X, ALU.max, negate=True)
                nc.vector.tensor_reduce(nm[:, hs, 1:2], src[:, :, N_TXT:N_BIG], AX_X, ALU.max, negate=True)
                nc.vector.tensor_reduce(nm[:, hs, 2:4], src[:, :, N_BIG:S].rearrange("p j (g t) -> p j g t", g=2),
                                        AX_X, ALU.max, negate=True).then_inc(s_max, 1)

            def split_maxima(a, b):
                n = 2 * a.i + b
                nm_v = nm[:, :, :].rearrange("p (f h) g -> p f (h g)", f=2)
                dve.wait_ge(s_max, NT * (n + 1))
                nc.vector.tensor_copy(mp[:, :, 0, :], nm_v).then_inc(m_chain, 1)
                dve.wait_ge(m_chain, 4 * n + 1)
                nc.vector.tensor_tensor(nmr[:, :, :], nm_v, mp[:, :, 0, :], ALU.subtract).then_inc(m_chain, 1)
                dve.wait_ge(m_chain, 4 * n + 2)
                nc.vector.tensor_copy(mp[:, :, 1, :], nmr[:, :, :]).then_inc(m_chain, 1)
                dve.wait_ge(m_chain, 4 * n + 3)
                nc.vector.tensor_tensor(mp[:, :, 2, :], nmr[:, :, :], mp[:, :, 1, :], ALU.subtract).then_inc(m_chain, 1)
                dve.wait_ge(m_chain, 4 * n + 4)
                nc.vector.tensor_copy(nmr2[:, 0, 0:1], nmr[:, 0, 0:1]).then_inc(m_parts, 1)

            def normalise(a, b, t, fresh):
                n = 2 * a.i + b
                bank = (n0(b) + t) % 2
                dve.wait_ge(pv_done, NT * n + t + 1)
                if t == 0 and not fresh and not (first_pair(a) and b == 1):
                    dve.wait_ge(o_sum, n - 1)
                o_v = ps_o[bank][:, 0:HT * OW].rearrange("p (j w) -> p j w", w=OW)
                nc.vector.reciprocal(rz[:, bank, :, :], o_v[:, :, G * HD:G * HD + G]).then_inc(z_inv, 1)
                dve.wait_ge(z_inv, NT * n + t + 1)
                nc.vector.tensor_tensor(og[:, b, t * HT:(t + 1) * HT, :, :].rearrange("p j g d -> p (j g) d"),
                                        o_v[:, :, 0:G * HD].rearrange("p j (g d) -> p j g d", g=G),
                                        rz[:, bank, :, :].rearrange("p j (g o) -> p j g o", o=1).to_broadcast([128, HT, G, HD]),
                                        ALU.mult).then_inc(o_norm, 1)

            def result(n, b_ring):
                bank, b = (b_ring * (NT + 2) + 1) % 2, 1 - b_ring
                dve.wait_ge(out_done, n)
                dve.wait_ge(xb_done, n)
                flat = ps_t[bank][:, :, :].rearrange("p j t -> p (j t)")
                nc.vector.tensor_tensor(res[:, b, :], flat[:, 0:C], xb[:, b, :], ALU.add).then_inc(res_done, 1)

            def step(q, a, first=False):
                for b in range(2):
                    fresh = first and b == 0
                    if a is not None:
                        maxima(a, b, 0, fresh)
                        maxima(a, b, 1, fresh)
                    if q is not None and b == 0:
                        q_low(q, 0)
                    if a is not None:
                        maxima(a, b, 2, fresh)
                        maxima(a, b, 3, fresh)
                    if q is not None and b == 0:
                        q_low(q, 1)
                    if a is not None:
                        maxima(a, b, 4, fresh)
                        split_maxima(a, b)
                        if not fresh:
                            if b == 1 and not first:
                                dve.wait_ge(stored[0], 16 * a.i)
                            if b == 0 and not second_pair(a):
                                dve.wait_ge(stored[1], 16 * (a.i - 1))
                            result(2 * a.i + b, b)
                    if q is not None and b == 0:
                        k_low(q, 0)
                        k_low(q, 1)
                    if a is not None:
                        for t in range(NT):
                            normalise(a, b, t, fresh)

            nc.vector.memset(ps_p[0][:, :], 0.0).then_inc(casts, 1)
            dve.wait_ge(sm_hi, 1)
            nc.vector.tensor_tensor(ksr[:, :, :, :].rearrange("p c b r -> p (c b r)"), ps_p[0][:, 0:384],
                                    ksm[:, 0, :, :, :].rearrange("p c b r -> p (c b r)"), ALU.subtract).then_inc(sm_rest, 1)
            step(pair(0), None)
            dve.wait_ge(consts, 48)
            nc.vector.tensor_copy(identb[:, :], ident[:, :]).then_inc(casts, 1)
            nc.vector.tensor_copy(sel[:, :, :].rearrange("p j k -> p (j k)"), sel_f[:, :]).then_inc(casts, 1)
            step(pair(1), pair(0), first=True)
            step(pair(2), pair(1))
            step(pair(3), pair(2))
            with dve.Fori(0, (PAIRS - 4) // 2) as j:
                step(Pair(4 + 2 * j, 0, 2 + j), Pair(3 + 2 * j, 1, 1 + j))
                step(Pair(5 + 2 * j, 1, 2 + j), Pair(4 + 2 * j, 0, 2 + j))
            step(None, pair(PAIRS - 1))
            dve.wait_ge(stored[1], 16 * (PAIRS - 1))
            result(B, 0)

        @block.gpsimd
        def _(pool):
            def sum_groups(n, b):
                pool.wait_ge(o_norm, NT * (n + 1))
                g_v = og[:, b, :, :, :].rearrange("p h (x y) d -> p h x (y d)", x=2)
                s_v = os[:, :, :, :].rearrange("p h y d -> p h (y d)")
                nc.gpsimd.tensor_tensor(s_v, g_v[:, :, 0, :], g_v[:, :, 1, :], ALU.add).then_inc(o_half, 1)
                pool.wait_ge(o_half, n + 1)
                nc.gpsimd.tensor_tensor(on[:, b, :].rearrange("p (h d) -> p h d", d=HD), os[:, :, 0, :], os[:, :, 1, :],
                                        ALU.add).then_inc(o_sum, 1)

            def add_bias(a, b):
                pool.wait_ge(xn_in[b], 16 * (a + 1))
                nc.gpsimd.tensor_tensor(xb[:, b, :], xn_sb[:, b, :], bias[:, :], ALU.add).then_inc(xb_done, 1)

            def q_split(q):
                for c in range(2):
                    rows, cs = (128, slice(0, 2)) if c == 0 else (XC[2], slice(2, 3))
                    pool.wait_ge(q_mid, 2 * q.i + 1 + c)
                    nc.gpsimd.tensor_tensor(qp[0:rows, 2, cs, :], qr[0:rows, cs, :], qp[0:rows, 1, cs, :],
                                            ALU.subtract).then_inc(q_parts, 1)

            def k_split(q):
                for c in range(2):
                    rows, cs = (128, slice(0, 2)) if c == 0 else (XC[2], slice(2, 3))
                    def view(x):
                        return x.rearrange("p c b t -> p (c b) t")
                    rest = view(kr[0:rows, cs, :, :])
                    mid = view(kp[0:rows, 1, cs, :, 0:N_BIG])
                    pool.wait_ge(k_mid, 2 * q.i + 1 + c)
                    nc.gpsimd.tensor_tensor(view(kp[0:rows, 2, cs, :, 0:N_BIG]), rest, mid, ALU.subtract).then_inc(k_parts, 1)

            def step(q, a, first=False):
                for b in range(2):
                    if a is not None and not (first and b == 0):
                        n = 2 * a.i + b - 1
                        if not (first or (second_pair(a) and b == 0)):
                            pool.wait_ge(ot_done, n - 1)
                            pool.wait_ge(res_done, n - 1)
                        sum_groups(n, 1 - b)
                        add_bias(a.i - (1 - b), 1 - b)
                    if q is not None and b == 0:
                        q_split(q)
                        k_split(q)

            pool.wait_ge(sm_rest, 1)
            nc.gpsimd.tensor_copy(ksm[:, 1, :, :, :], ksr[:, :, :, :]).then_inc(sm_mid, 1)
            pool.wait_ge(sm_mid, 1)
            nc.gpsimd.tensor_tensor(ksm[:, 2, :, :, :], ksr[:, :, :, :], ksm[:, 1, :, :, :], ALU.subtract).then_inc(sm_parts, 1)
            pool.wait_ge(sm_parts, 1)
            step(pair(0), None)
            pool.wait_ge(consts, 48)
            step(pair(1), pair(0), first=True)
            step(pair(2), pair(1))
            step(pair(3), pair(2))
            with pool.Fori(0, (PAIRS - 4) // 2) as j:
                step(Pair(4 + 2 * j, 0, 2 + j), Pair(3 + 2 * j, 1, 1 + j))
                step(Pair(5 + 2 * j, 1, 2 + j), Pair(4 + 2 * j, 0, 2 + j))
            step(None, pair(PAIRS - 1))
            pool.wait_ge(ot_done, B - 2)
            sum_groups(B - 1, 1)
            pool.wait_ge(res_done, B - 2)
            add_bias(PAIRS - 1, 1)


def n0(b):
    return b * NT


def first_pair(a):
    return isinstance(a.i, int) and a.i == 0


def second_pair(a):
    return isinstance(a.i, int) and a.i == 1


def kernel(**inputs):
    import concourse.bacc as _bacc
    from concourse.bass_utils import run_bass_kernel_spmd as _run

    x = np.asarray(inputs["x"])
    ctx = np.asarray(inputs["ctx_2048"])
    w = {k: np.asarray(v) for k, v in inputs.items() if k.startswith("L0_xattn_")}
    p = "L0_xattn_to_"
    cols = [(2 * h + c) * HD + d for c in range(2) for d in range(HD) for h in range(8)]
    cols += [(16 + h) * HD + d for d in range(HD) for h in range(H - 16)]
    xT = np.ascontiguousarray(x.reshape(PAIRS, T2, C).transpose(0, 2, 1))
    e = [0, N_TXT, N_TXT + N_OBJ, N_TXT + N_OBJ + N_OTH, S]
    grp = [ctx[:, e[g]:e[g + 1], :] for g in range(G)]
    big = [grp[g].reshape(PAIRS, -1, CA) for g in (0, 3)]
    cM = np.ascontiguousarray(np.concatenate(big, axis=1).transpose(0, 2, 1))
    cS = np.ascontiguousarray(np.concatenate([grp[g].reshape(-1, CA) for g in (1, 2)], axis=0).T)
    group_of = np.repeat(np.arange(G), [N_TXT, N_IP, N_OBJ, N_OTH])
    sel = np.zeros((3, HH, G, HH, S), np.float32)
    spread = np.zeros((S, G + 1, H, HD), np.float32)
    for g in range(G):
        for h in range(HH):
            sel[:, h, g, h, group_of == g] = 1.0
        spread[group_of == g, G, :, g] = 1.0
    arrays = {
        "xT": xT, "xn": np.ascontiguousarray(x.reshape(B * S, C)), "cM": cM, "cS": cS,
        "wq": np.ascontiguousarray(w[p + "q_w"][:, cols]),
        "wkt": np.ascontiguousarray(w[p + "k_w"][:, cols]), "wvt": w[p + "v_w"],
        "wki": np.ascontiguousarray(w[p + "k_ip_w"][:, cols]), "wvi": w[p + "v_ip_w"],
        "wko": np.ascontiguousarray(w[p + "k_object_w"][:, cols]), "wvo": w[p + "v_object_w"],
        "wkh": np.ascontiguousarray(w[p + "k_others_w"][:, cols]), "wvh": w[p + "v_others_w"],
        "wo": w[p + "out_w"], "bo": w[p + "out_b"],
        "ident": np.eye(128, dtype=np.float32), "sel": sel.reshape(MR, HH * S), "spread": spread.reshape(S, VB),
    }
    nc = _bacc.Bacc("TRN2", target_bir_lowering=False, num_devices=1)
    args = []
    for name, a in arrays.items():
        args.append(nc.dram_tensor("in_" + name, a.shape, F32, kind="ExternalInput").ap())
    out = nc.dram_tensor("out_0", (B * S, C), F32, kind="ExternalOutput").ap()
    build(nc, *args, out)
    r = _run(nc, [{"in_" + k: v for k, v in arrays.items()}], core_ids=[0])
    return r.results[0]["out_0"].reshape(B, S, C)
```

```python
from contextlib import ExitStack

import numpy as np

import concourse.bass as bass
from concourse import mybir

F32 = mybir.dt.float32
F32R = mybir.dt.float32r
BF16 = mybir.dt.bfloat16
ALU = mybir.AluOpType
ACT = mybir.ActivationFunctionType
AX_X = mybir.AxisListType.X

B, S, C, CA = 16, 128, 320, 512
H, HD = 20, 16
G = 4
N_TXT, N_OBJ, N_OTH = 77, 4, 4
N_IP = S - N_TXT - N_OBJ - N_OTH
N_BIG = N_TXT + N_IP
N_SML = N_OBJ
PAIRS = B // 2
T2 = 2 * S
SCALE = 1.0 / float(np.sqrt(HD))
KC = CA // 128
XC = [128, 128, C - 256]
HT = 4
NT = H // HT
SLOTS_Q = [0, 0, 0, 1, 1, 2]
SLOTS_K = [0, 1, 2, 0, 1, 0]
KS = 16 * len(SLOTS_Q)
HH = H // 2
MS = 3 * G
MR = MS * HH
OW = (G + 1) * HD
RELAY = 12 * 16
N_VDMA = 4 * 16


class Pair:

    def __init__(self, index, parity, use):
        self.i, self.par, self.use = index, parity, use


def pair(i):
    return Pair(i, i % 2, i // 2)


def build(nc, xT, xn, cM, cS, wq, wkt, wvt, wki, wvi, wko, wvo, wkh, wvh, wo, bo, ident_d, krow_d, ind_d, out):
    ctx = ExitStack()
    with ctx:
        def sb(name, shape, dt=F32):
            return ctx.enter_context(nc.sbuf_tensor(name, shape, dt))

        def ps(name, shape):
            return ctx.enter_context(nc.psum_tensor(name, shape, F32))

        def sem(name):
            return ctx.enter_context(nc.semaphore(name))

        wq_sb = sb("wq_sb", [128, 3, C])
        wo_sb = sb("wo_sb", [128, 3, C])
        wk_sb = [sb(f"wk_sb{g}", [128, KC, C]) for g in range(2)]
        wv_sb = [sb(f"wv_sb{g}", [128, KC, C]) for g in range(2)]
        wks_then_pT = sb("wks_then_pT", [128, 2 * KC * C])
        wvs_then_og = sb("wvs_then_og", [128, 2 * KC * C])
        wks_sb = wks_then_pT[:, :].rearrange("p (g k n) -> p g k n", g=2, k=KC)
        wvs_sb = wvs_then_og[:, :].rearrange("p (g k n) -> p g k n", g=2, k=KC)
        bias = sb("bias", [128, C])
        ident = sb("ident", [128, 128])
        identb = sb("identb", [128, 128], BF16)
        krow_f = sb("krow_f", [MS, T2])
        krow = sb("krow", [MS, T2], BF16)
        wq_h = [sb(f"wq_h{k}", [128, 3, C], F32R) for k in range(2)]
        wv_h = [[sb(f"wv_h{g}{k}", [128, KC, C], F32R) for k in range(2)] for g in range(2)]
        xT_sb = sb("xT_sb", [128, 2, 3, T2])
        cT_sb = sb("cT_sb", [128, 2, KC, 2 * N_BIG])
        xT_h = [sb(f"xT_h{k}", [128, 3, T2], F32R) for k in range(2)]
        cT_h = [sb(f"cT_h{k}", [128, KC, 2 * N_BIG], F32R) for k in range(2)]
        cS_then_xb = sb("cS_then_xb", [128, 2 * C])
        cS_sb = cS_then_xb[:, 0:2 * KC * B * N_SML].rearrange("p (k r) -> p k r", k=KC)
        xn_sb = sb("xn_sb", [128, 2, C])
        xb = cS_then_xb[:, :].rearrange("p (b n) -> p b n", b=2)
        qp = sb("qp", [128, 3, 3, T2], BF16)
        kp = sb("kp", [128, 3, 3, 2, S], BF16)
        ksm = sb("ksm", [128, 3, 3, B, 2 * N_SML], BF16)
        qr = sb("qr", [128, 3, T2])
        kr = sb("kr", [128, 3, 2, N_BIG])
        qst = [sb(f"qst{p}", [KS + MS, H, T2], BF16) for p in range(2)]
        kst = [sb(f"kst{p}", [KS + MS, H, T2], BF16) for p in range(2)]
        vbd = sb("vbd", [128, 2, 2, G + 1, C])
        vip = sb("vip", [2 * N_IP, C])
        vsm_then_os = sb("vsm_then_os", [128, 2 * C])
        vsm = vsm_then_os[0:B * N_SML, :].rearrange("p (g n) -> p g n", g=2)
        vs_dram = nc.dram_tensor("vs_dram", (PAIRS, 2, 2 * N_SML, C), F32, kind="Internal").ap()
        nm = sb("nm", [128, H, G])
        nmr = sb("nmr", [128, 2, G, HH])
        mp = sb("mp", [128, 2, 3, G, HH], BF16)
        mT = sb("mT", [MR, 2, 128], BF16)
        pT = wks_then_pT[:, :].rearrange("p (t j s) -> p t j s", t=NT, j=HT)
        rz = sb("rz", [128, 2, HT, G])
        og = wvs_then_og[:, :].rearrange("p (b h g d) -> p b h g d", b=2, h=H, g=G)
        os = vsm_then_os[:, :].rearrange("p (h y d) -> p h y d", h=H, y=2)
        on = sb("on", [128, 2, H * HD])
        ksr_then_oT = sb("ksr_then_oT", [128, 2 * 3 * 128])
        ksr = ksr_then_oT[:, 0:3 * 2 * B * N_SML].rearrange("p (c b r) -> p c b r", c=3, b=B)
        oT = ksr_then_oT[:, :].rearrange("p (b c q) -> p b c q", b=2, c=3)
        res = sb("res", [128, 2, C])

        ps_s = [ps(f"ps_s{k}", [128, HT, S]) for k in range(2)]
        ps_t = [ps(f"ps_t{k}", [128, HT, S]) for k in range(2)]
        ps_o = [ps(f"ps_o{k}", [128, 512]) for k in range(2)]
        ps_p = [ps(f"ps_p{k}", [128, 512]) for k in range(2)]

        w_ks, w_vs, w_q, w_k, w_v, w_o = (sem(n) for n in ("w_ks", "w_vs", "w_q", "w_k", "w_v", "w_o"))
        consts, zeros, spread_in, krow_in = sem("consts"), sem("zeros"), sem("spread_in"), sem("krow_in")
        w_hi, w_lo, x_hi, x_lo, c_hi, c_lo = (sem(n) for n in ("w_hi", "w_lo", "x_hi", "x_lo", "c_hi", "c_lo"))
        x_in = [sem(f"x_in{p}") for p in range(2)]
        c_in = [sem(f"c_in{p}") for p in range(2)]
        xn_in = [sem(f"xn_in{b}") for b in range(2)]
        casts = sem("casts")
        q_done, k_done, v_done = sem("q_done"), sem("k_done"), sem("v_done")
        q_hi, k_hi, q_rest, k_rest = sem("q_hi"), sem("k_hi"), sem("q_rest"), sem("k_rest")
        q_mid, k_mid, k_small = sem("q_mid"), sem("k_mid"), sem("k_small")
        q_parts, k_parts = sem("q_parts"), sem("k_parts")
        q_st = [sem(f"q_st{p}") for p in range(2)]
        k_st = [sem(f"k_st{p}") for p in range(2)]
        v_put, vip_out = sem("v_put"), sem("vip_out")
        v_in = [sem(f"v_in{p}") for p in range(2)]
        s_done, s_max, m_chain, m_parts = sem("s_done"), sem("s_max"), sem("m_chain"), sem("m_parts")
        mt_done, mt_out, m_st = sem("mt_done"), sem("mt_out"), sem("m_st")
        t_done, t_exp, pv_done = sem("t_done"), sem("t_exp"), sem("pv_done")
        z_inv, o_norm, o_half, o_sum = sem("z_inv"), sem("o_norm"), sem("o_half"), sem("o_sum")
        ot_done, ot_out, out_done, xb_done, res_done = (
            sem(n) for n in ("ot_done", "ot_out", "out_done", "xb_done", "res_done"))
        stored = [sem(f"stored{b}") for b in range(2)]
        sm_k, sm_v, sm_hi, sm_rest, sm_mid, sm_parts, sm_vout, sm_dram = (
            sem(n) for n in ("sm_k", "sm_v", "sm_hi", "sm_rest", "sm_mid", "sm_parts", "sm_vout", "sm_dram"))

        block = ctx.enter_context(nc.Block())

        @block.sync
        def _(sp):
            xn_v = xn.rearrange("(p b q) n -> p b q n", b=2, q=S)
            out_v = out.rearrange("(p b q) n -> p b q n", b=2, q=S)

            def addresses(i, *tensors):
                if not isinstance(i, int):
                    for t in tensors:
                        sp.snap(i * (t.size() // t.shape[0]) * 4)

            def load_x_turned(i, p):
                sp.dma_start(xT_sb[:, p, 0:2, :], xT[i, 0:256, :].rearrange("(k p) t -> p k t", p=128)).then_inc(x_in[p], 16)
                sp.dma_start(xT_sb[0:XC[2], p, 2, :], xT[i, 256:C, :]).then_inc(x_in[p], 16)

            def load_tokens(i, p):
                load_x_turned(i, p)
                sp.dma_start(cT_sb[:, p, :, :], cM[i].rearrange("(k p) t -> p k t", p=128)).then_inc(c_in[p], 16)

            def load_next(q):
                addresses(q.i, xT, cM)
                sp.wait_ge(v_done, 3 * (q.i - 1))
                load_tokens(q.i, q.par)

            def stack(q, parts, slots, to, part_done, done):
                for c in range(2):
                    for part in range(3):
                        sp.wait_ge(part_done[part], 2 * q.i + 1 + c)
                        for n in [n for n in range(len(slots)) if slots[n] == part]:
                            rows = slice(16 * n, 16 * n + 16)
                            if c == 0:
                                sp.dma_start(to[q.par][rows, 0:16, :], parts[:, part, 0:2, :]).then_inc(done[q.par], 16)
                            else:
                                sp.dma_start(to[q.par][rows, 16:H, :], parts[0:XC[2], part, 2, :]).then_inc(done[q.par], 16)

            kp_v = kp[:, :, :, :, :].rearrange("p a c b t -> p a c (b t)")

            def stack_q(q):
                stack(q, qp, SLOTS_Q, qst, (q_hi, q_mid, q_parts), q_st)

            def stack_k(q):
                sp.wait_ge(k_small, 2 * q.i + 1)
                stack(q, kp_v, SLOTS_K, kst, (k_hi, k_mid, k_parts), k_st)

            def spread_v(q):
                for g in range(2):
                    k0 = N_BIG + g * N_SML
                    sp.dma_start(vbd[k0:k0 + N_SML, q.par, :, 2 + g, :],
                                 vs_dram[q.i, :, g * N_SML:(g + 1) * N_SML, :].rearrange("b t n -> t b n"))\
                      .then_inc(v_in[q.par], 16)
                sp.wait_ge(vip_out, q.i + 1)
                for b in range(2):
                    sp.dma_start(vbd[N_TXT:N_BIG, q.par, b, 1, :], vip[b * N_IP:(b + 1) * N_IP, :])\
                      .then_inc(v_in[q.par], 16)

            def load_x(a, b):
                sp.dma_start(xn_sb[:, b, :], xn_v[a, b]).then_inc(xn_in[b], 16)

            def store(a, b):
                sp.wait_ge(res_done, 2 * a + b + 1)
                sp.dma_start(out_v[a, b], res[:, b, :]).then_inc(stored[b], 16)

            def step(q, a, first=False):
                if a is not None:
                    if not first:
                        sp.wait_ge(xb_done, 2 * a - 1)
                    load_x(a, 0)
                if q is not None:
                    stack_k(q)
                    stack_q(q)
                if a is not None:
                    if not first:
                        store(a - 1, 1)
                        sp.wait_ge(xb_done, 2 * a)
                    load_x(a, 1)
                if q is not None:
                    if not (isinstance(q.i, int) and q.i < 2):
                        sp.wait_ge(pv_done, 2 * NT * (q.i - 1))
                    spread_v(q)
                if a is not None:
                    store(a, 0)

            sp.dma_start(cS_sb[:, :, :], cS.rearrange("(k p) t -> p k t", p=128)).then_inc(w_ks, 16)
            for g, wk in enumerate((wko, wkh)):
                sp.dma_start(wks_sb[:, g, :, :], wk.rearrange("(k p) n -> p k n", p=128)).then_inc(w_ks, 16)
            sp.dma_start(cT_sb[:, 0, :, :], cM[0].rearrange("(k p) t -> p k t", p=128)).then_inc(c_in[0], 16)
            for g, wk in enumerate((wkt, wki)):
                sp.dma_start(wk_sb[g][:, :, :], wk.rearrange("(k p) n -> p k n", p=128)).then_inc(w_k, 16)
            sp.dma_start(wq_sb[:, 0:2, :], wq[0:256, :].rearrange("(k p) n -> p k n", p=128)).then_inc(w_q, 16)
            sp.dma_start(wq_sb[0:XC[2], 2, :], wq[256:C, :]).then_inc(w_q, 16)
            load_x_turned(0, 0)
            for g, wv in enumerate((wvo, wvh)):
                sp.dma_start(wvs_sb[:, g, :, :], wv.rearrange("(k p) n -> p k n", p=128)).then_inc(w_vs, 16)
            for g, wv in enumerate((wvt, wvi)):
                sp.dma_start(wv_sb[g][:, :, :], wv.rearrange("(k p) n -> p k n", p=128)).then_inc(w_v, 16)
            sp.dma_start(ident[:, :], ident_d).then_inc(consts, 16)
            sp.dma_start(krow_f[:, :], krow_d).then_inc(consts, 16)
            sp.dma_start(bias[:, :], bo.partition_broadcast(128)).then_inc(consts, 16)
            for p in range(2):
                for b in range(2):
                    sp.dma_start(vbd[:, p, b, G, :], ind_d).then_inc(spread_in, 16)
            load_tokens(1, 1)
            sp.dma_start(wo_sb[:, 0:2, :], wo[0:256, :].rearrange("(k p) n -> p k n", p=128)).then_inc(w_o, 16)
            sp.dma_start(wo_sb[0:XC[2], 2, :], wo[256:C, :]).then_inc(w_o, 16)
            sp.wait_ge(casts, 3)
            for p in range(2):
                sp.dma_start(kst[p][KS:KS + MS, :, :], krow[:, :].rearrange("r (o t) -> r o t", o=1)
                             .to_broadcast([MS, H, T2])).then_inc(krow_in, 16)
            stack_k(pair(0))
            stack_q(pair(0))
            sp.wait_ge(sm_vout, 2)
            for g in range(2):
                sp.dma_start(vs_dram.rearrange("p b r n -> (p b) r n")[:, g * N_SML:(g + 1) * N_SML, :],
                             vsm[:, g, :]).then_inc(sm_dram, 16)
            sp.wait_ge(sm_dram, 32)
            sp.wait_ge(zeros, 1)
            spread_v(pair(0))
            load_next(pair(2))
            step(pair(1), 0, first=True)
            load_next(pair(3))
            step(pair(2), 1)
            with sp.Fori(0, (PAIRS - 4) // 2) as j:
                load_next(Pair(4 + 2 * j, 0, 2 + j))
                step(Pair(3 + 2 * j, 1, 1 + j), 2 + 2 * j)
                load_next(Pair(5 + 2 * j, 1, 2 + j))
                step(Pair(4 + 2 * j, 0, 2 + j), 3 + 2 * j)
            step(pair(PAIRS - 1), PAIRS - 2)
            step(None, PAIRS - 1)
            store(PAIRS - 1, 1)
            for b in range(2):
                sp.wait_ge(stored[b], 16 * PAIRS)

        @block.tensor
        def _(pe):
            def passes(q, plain, halves, m):
                if isinstance(q.i, int) and q.i == 0:
                    return [plain]
                (s, t) = halves
                return [(s[0], t[0]), (s[0], t[1]), (s[1], t[0])]

            def q_chunk(q, to, c):
                w, pairs = XC[c], passes(q, (wq_sb, xT_sb[:, q.par, :, :]), (wq_h, [x[:, :, :] for x in xT_h]), None)
                n = 0
                for wt, xt in pairs:
                    for k in range(3):
                        mm = nc.tensor.matmul(to, wt[0:XC[k], k, c * 128:c * 128 + w], xt[0:XC[k], k, :],
                                              start=(n == 0), stop=(n == 3 * len(pairs) - 1))
                        n += 1
                return mm

            def project_q01(q):
                pe.wait_ge(k_rest, 2 * q.i + 1)
                if isinstance(q.i, int) and q.i == 0:
                    pe.wait_ge(w_q, 32)
                    pe.wait_ge(x_in[0], 32)
                else:
                    pe.wait_ge(x_lo, 2 * q.i)
                for c in range(2):
                    mm = q_chunk(q, ps_p[0][:, c * T2:(c + 1) * T2], c)
                mm.then_inc(q_done, 1)

            def project_q2(q):
                pe.wait_ge(k_rest, 2 * q.i + 2)
                q_chunk(q, ps_p[1][0:XC[2], 0:T2], 2).then_inc(q_done, 1)

            def k_chunk(q, bank, at, c):
                w = XC[c]
                view = ps_p[bank][0:w, at:at + T2].rearrange("p (b t) -> p b t", b=2)
                for g, (t0, n) in enumerate(((0, N_TXT), (N_TXT, N_IP))):
                    rhs = cT_sb[:, q.par, :, 2 * t0:2 * (t0 + n)].rearrange("p k (b t) -> p k b t", b=2)
                    for k in range(KC):
                        mm = nc.tensor.matmul(view[:, :, t0:t0 + n], wk_sb[g][:, k, c * 128:c * 128 + w],
                                              rhs[:, k, :, :], start=(k == 0), stop=(k == KC - 1))
                return mm

            def project_k01(q):
                pe.wait_ge(c_in[q.par], 16 * (q.use + 1))
                if not (isinstance(q.i, int) and q.i == 0):
                    pe.wait_ge(vip_out, q.i)
                k_chunk(q, 0, 0, 0)
                k_chunk(q, 0, T2, 1).then_inc(k_done, 1)

            def project_k2(q):
                if not (isinstance(q.i, int) and q.i == 0):
                    pe.wait_ge(v_put, 2 * q.i)
                k_chunk(q, 1, 0, 2).then_inc(k_done, 1)

            def project_v(q, n):
                if n < 2:
                    pe.wait_ge(q_rest, 2 * q.i + 1 + n)
                else:
                    pe.wait_ge(v_put, 2 * q.i + 1)
                if n == 0 and not (isinstance(q.i, int) and q.i == 0):
                    pe.wait_ge(c_lo, q.i)
                t0, m = [(0, N_TXT), (N_TXT, N_TXT), (2 * N_TXT, 2 * N_IP)][n]
                pairs = passes(q, (cT_sb[:, q.par, :, :], wv_sb[n // 2]), ([c[:, :, :] for c in cT_h], wv_h[n // 2]), m)
                left = KC * len(pairs)
                for ct, wt in pairs:
                    for k in range(KC):
                        mm = nc.tensor.matmul(ps_p[n % 2][0:m, 0:C], ct[:, k, t0:t0 + m], wt[:, k, :],
                                              start=(left == KC * len(pairs)), stop=(left == 1))
                        left -= 1
                mm.then_inc(v_done, 1)

            def score_tile(a, b, t, fresh):
                n = 2 * a.i + b
                if t >= 2:
                    pe.wait_ge(s_max, NT * n + t - 1)
                elif not fresh:
                    if t == 0:
                        pe.wait_ge(s_max, NT * n)
                    else:
                        pe.wait_ge(mt_out, n)
                for j in range(HT):
                    h = t * HT + j
                    mm = nc.tensor.matmul(ps_s[t % 2][:, j, :], qst[a.par][0:KS, h, b * S:(b + 1) * S],
                                          kst[a.par][0:KS, h, b * S:(b + 1) * S], start=True, stop=True)
                mm.then_inc(s_done, 1)

            def turn_maxima(a, b):
                n = 2 * a.i + b
                pe.wait_ge(m_parts, n + 1)
                for half in range(2):
                    mm = nc.tensor.matmul(ps_s[1][0:MR, half, :], mp[:, half, :, :, :].rearrange("p a g h -> p (a g h)"),
                                          identb[:, :], start=True, stop=True)
                mm.then_inc(mt_done, 1)

            def exp_tile(a, b, t, fresh):
                n = 2 * a.i + b
                bank = t_bank(b, 1 + t)
                if t >= 2:
                    pe.wait_ge(t_exp, NT * n + t - 1)
                elif not fresh:
                    if t == 1:
                        pe.wait_ge(ot_out, n)
                    elif not (first_pair(a) and b == 1):
                        pe.wait_ge(res_done, n - 1)
                if t == 0:
                    pe.wait_ge(m_st, 16 * (n + 1))
                for j in range(HT):
                    h = t * HT + j
                    mm = nc.tensor.matmul(ps_t[bank][:, j, :], kst[a.par][:, h, b * S:(b + 1) * S],
                                          qst[a.par][:, h, b * S:(b + 1) * S], start=True, stop=True)
                mm.then_inc(t_done, 1)

            def value_tile(a, b, t, fresh):
                n = 2 * a.i + b
                bank = (n0(b) + t) % 2
                if not (fresh and t < 2):
                    pe.wait_ge(o_norm, NT * n + t - 1)
                if t == 0:
                    pe.wait_ge(v_put, 2 * (a.i + 1))
                    pe.wait_ge(v_in[a.par], N_VDMA * (a.use + 1))
                pe.wait_ge(t_exp, NT * n + t + 1)
                for j in range(HT):
                    h = t * HT + j
                    mm = nc.tensor.matmul(ps_o[bank][:, j * OW:(j + 1) * OW], pT[:, t, j, :],
                                          vbd[:, a.par, b, :, h * HD:(h + 1) * HD], start=True, stop=True)
                mm.then_inc(pv_done, 1)

            def turn_heads(n, b):
                pe.wait_ge(t_exp, NT * n)
                pe.wait_ge(o_sum, n)
                flat = ps_t[t_bank(b, 0)][:, :, :].rearrange("p j t -> p (j t)")
                for c in range(3):
                    mm = nc.tensor.transpose(flat[0:XC[c], c * 128:(c + 1) * 128],
                                             on[:, 1 - b, c * 128:c * 128 + XC[c]], ident[:, :])
                mm.then_inc(ot_done, 1)

            def output(n, b, last=False):
                if not last:
                    pe.wait_ge(t_exp, NT * n + NT - 1)
                pe.wait_ge(ot_out, n)
                flat = ps_t[t_bank(b, NT + 1)][:, :, :].rearrange("p j t -> p (j t)")
                for c in range(3):
                    mm = nc.tensor.matmul(flat[:, 0:C], oT[0:XC[c], 1 - b, c, :], wo_sb[0:XC[c], c, :],
                                          start=(c == 0), stop=(c == 2))
                mm.then_inc(out_done, 1)

            def attend(a, b, fresh, nxt, nb):
                n = 2 * a.i + b
                if nxt is not None:
                    if nb == 0:
                        pe.wait_ge(q_st[nxt.par], RELAY * (nxt.use + 1))
                        pe.wait_ge(k_st[nxt.par], RELAY * (nxt.use + 1))
                    score_tile(nxt, nb, 0, False)
                    score_tile(nxt, nb, 1, False)
                for t in range(NT):
                    value_tile(a, b, t, fresh)
                    if t + 2 < NT:
                        exp_tile(a, b, t + 2, fresh)
                        if nxt is not None:
                            score_tile(nxt, nb, t + 2, False)
                if not fresh:
                    output(n, b)
                if nxt is not None:
                    turn_maxima(nxt, nb)

            def step(q, a, first=False):
                if q is not None:
                    project_k01(q)
                    project_k2(q)
                if not first:
                    turn_heads(2 * a.i, 0)
                exp_tile(a, 0, 0, first)
                if q is not None:
                    project_q01(q)
                exp_tile(a, 0, 1, first)
                if q is not None:
                    project_q2(q)
                attend(a, 0, first, a, 1)
                if q is not None:
                    project_v(q, 0)
                    project_v(q, 1)
                turn_heads(2 * a.i + 1, 1)
                if q is not None:
                    project_v(q, 2)
                for t in range(2):
                    exp_tile(a, 1, t, False)
                attend(a, 1, False, q, 0)

            pe.wait_ge(w_ks, 48)
            pe.wait_ge(casts, 1)
            small_k = ps_s[0][:, :, :].rearrange("p j t -> p (j t)")
            for g in range(2):
                for c in range(3):
                    w = XC[c]
                    view = small_k[0:w, c * 128:(c + 1) * 128].rearrange("p (b r) -> p b r", b=B)
                    rhs = cS_sb[:, :, g * B * N_SML:(g + 1) * B * N_SML].rearrange("p k (b t) -> p k b t", b=B)
                    for k in range(KC):
                        mm = nc.tensor.matmul(view[:, :, g * N_SML:(g + 1) * N_SML],
                                              wks_sb[:, g, k, c * 128:c * 128 + w], rhs[:, k, :, :],
                                              start=(k == 0), stop=(k == KC - 1))
            mm.then_inc(sm_k, 1)
            pe.wait_ge(w_k, 32)
            project_k01(pair(0))
            project_k2(pair(0))
            project_q01(pair(0))
            project_q2(pair(0))
            pe.wait_ge(w_vs, 32)
            for g in range(2):
                for k in range(KC):
                    mm = nc.tensor.matmul(ps_o[g][0:B * N_SML, 0:C], cS_sb[:, k, g * B * N_SML:(g + 1) * B * N_SML],
                                          wvs_sb[:, g, k, :], start=(k == 0), stop=(k == KC - 1))
                mm.then_inc(sm_v, 1)
            pe.wait_ge(w_v, 32)
            for n in range(3):
                project_v(pair(0), n)
            pe.wait_ge(sm_rest, 1)
            pe.wait_ge(sm_vout, 2)
            pe.wait_ge(q_st[0], RELAY)
            pe.wait_ge(k_st[0], RELAY)
            for t in range(NT):
                score_tile(pair(0), 0, t, True)
            pe.wait_ge(casts, 2)
            turn_maxima(pair(0), 0)
            pe.wait_ge(consts, 48)
            pe.wait_ge(spread_in, 64)
            pe.wait_ge(krow_in, 32)
            pe.wait_ge(w_lo, 4)
            pe.wait_ge(w_o, 32)
            step(pair(1), pair(0), first=True)
            with pe.Fori(0, (PAIRS - 2) // 2) as j:
                step(Pair(2 + 2 * j, 0, 1 + j), Pair(1 + 2 * j, 1, j))
                step(Pair(3 + 2 * j, 1, 1 + j), Pair(2 + 2 * j, 0, 1 + j))
            step(None, pair(PAIRS - 1))
            turn_heads(B, 0)
            output(B, 0, last=True)

        @block.scalar
        def _(act):
            def q_high(q, c):
                act.wait_ge(q_done, 2 * q.i + 1 + c)
                if c == 0:
                    if not (isinstance(q.i, int) and q.i == 0):
                        act.wait_ge(q_st[1 - q.par], RELAY * (q.use + q.par))
                    nc.scalar.activation(qp[:, 0, 0:2, :].rearrange("p c t -> p (c t)"), ps_p[0][:, :],
                                         ACT.Copy).then_inc(q_hi, 1)
                else:
                    nc.scalar.activation(qp[0:XC[2], 0, 2, :], ps_p[1][0:XC[2], 0:T2], ACT.Copy).then_inc(q_hi, 1)

            def k_high(q, c):
                act.wait_ge(k_done, 2 * q.i + 1 + c)
                if c == 0:
                    if not (isinstance(q.i, int) and q.i == 0):
                        act.wait_ge(k_st[1 - q.par], RELAY * (q.use + q.par))
                    src = ps_p[0][:, :].rearrange("p (m t) -> p m t", t=S)
                    dst = kp[:, 0, 0:2, :, :].rearrange("p c b t -> p (c b) t")
                    nc.scalar.activation(dst[:, :, 0:N_BIG], src[:, :, 0:N_BIG], ACT.Copy).then_inc(k_hi, 1)
                    small = ksm[:, :, :, :, :].rearrange("p a c (i b) r -> p i (a c) b r", b=2)
                    nc.scalar.activation(kp[:, :, :, :, N_BIG:S].rearrange("p a c b r -> p (a c) b r"),
                                         small[:, q.i, :, :, :], ACT.Copy).then_inc(k_small, 2)
                else:
                    src = ps_p[1][0:XC[2], 0:T2].rearrange("p (m t) -> p m t", t=S)
                    nc.scalar.activation(kp[0:XC[2], 0, 2, :, 0:N_BIG], src[:, :, 0:N_BIG], ACT.Copy).then_inc(k_hi, 1)

            def q_middle(q, c):
                act.wait_ge(q_rest, 2 * q.i + 1 + c)
                rows, cs = (128, slice(0, 2)) if c == 0 else (XC[2], slice(2, 3))
                nc.scalar.activation(qp[0:rows, 1, cs, :], qr[0:rows, cs, :], ACT.Copy).then_inc(q_mid, 1)

            def k_middle(q, c):
                act.wait_ge(k_rest, 2 * q.i + 1 + c)
                rows, cs = (128, slice(0, 2)) if c == 0 else (XC[2], slice(2, 3))
                nc.scalar.activation(kp[0:rows, 1, cs, :, 0:N_BIG].rearrange("p c b t -> p (c b) t"),
                                     kr[0:rows, cs, :, :].rearrange("p c b t -> p (c b) t"), ACT.Copy).then_inc(k_mid, 1)

            def v_text(q, b):
                act.wait_ge(v_done, 3 * q.i + 1 + b)
                nc.scalar.activation(vbd[0:N_TXT, q.par, b, 0, :], ps_p[b][0:N_TXT, 0:C], ACT.Copy).then_inc(v_put, 1)

            def v_image(q):
                act.wait_ge(v_done, 3 * q.i + 3)
                if not (isinstance(q.i, int) and q.i == 0):
                    act.wait_ge(v_in[1 - q.par], N_VDMA * (q.use + q.par))
                nc.scalar.activation(vip[:, :], ps_p[0][0:2 * N_IP, 0:C], ACT.Copy).then_inc(vip_out, 1)

            def heads_out(n, b):
                act.wait_ge(ot_done, n)
                flat = ps_t[t_bank(b, 0)][:, :, :].rearrange("p j t -> p (j t)")
                dst = oT[:, 1 - b, :, :].rearrange("p c t -> p (c t)")
                nc.scalar.activation(dst[:, 0:256], flat[:, 0:256], ACT.Copy)
                nc.scalar.activation(dst[0:XC[2], 256:384], flat[0:XC[2], 256:384], ACT.Copy).then_inc(ot_out, 1)

            def maxima_out(a, b):
                n = 2 * a.i + b
                act.wait_ge(mt_done, n + 1)
                if not (first_pair(a) and b == 0):
                    act.wait_ge(m_st, 16 * n)
                nc.scalar.activation(mT[:, :, :], ps_s[1][0:MR, 0:2, :], ACT.Copy).then_inc(mt_out, 1)
                act.wait_ge(mt_out, n + 1)
                act.dma_start(qst[a.par][KS:KS + MS, :, b * S:(b + 1) * S],
                              mT[:, :, :].rearrange("p f q -> p (f q)")).then_inc(m_st, 16)

            def exponentials(a, b, t, fresh):
                n = 2 * a.i + b
                bank = t_bank(b, 1 + t)
                act.wait_ge(t_done, NT * n + t + 1)
                if not fresh:
                    act.wait_ge(pv_done, NT * (n - 1) + t + 1)
                nc.scalar.activation(pT[:, t, :, :], ps_t[bank][:, :, :], ACT.Exp, scale=SCALE)\
                  .then_inc(t_exp, 1)

            def high_halves(q):
                act.wait_ge(x_in[q.par], 32 * (q.use + 1))
                act.wait_ge(q_done, 2 * q.i)
                nc.scalar.activation(xT_h[0][:, 0:2, :], xT_sb[:, q.par, 0:2, :], ACT.Copy).then_inc(x_hi, 1)
                nc.scalar.activation(xT_h[0][0:XC[2], 2, :], xT_sb[0:XC[2], q.par, 2, :], ACT.Copy).then_inc(x_hi, 1)

            def high_context(q):
                act.wait_ge(c_in[q.par], 16 * (q.use + 1))
                act.wait_ge(v_done, 3 * q.i)
                nc.scalar.activation(cT_h[0][:, :, :], cT_sb[:, q.par, :, :], ACT.Copy).then_inc(c_hi, 1)

            def attend(a, b, fresh, nxt, nb, middle=None):
                for t in range(2, NT):
                    exponentials(a, b, t, fresh)
                if middle is not None:
                    q_middle(middle, 1)
                if nxt is not None:
                    maxima_out(nxt, nb)

            def step(q, a, first=False):
                if q is not None:
                    high_halves(q)
                    high_context(q)
                    k_high(q, 0)
                    k_middle(q, 0)
                    k_high(q, 1)
                if not first:
                    heads_out(2 * a.i, 0)
                if q is not None:
                    k_middle(q, 1)
                exponentials(a, 0, 0, first)
                if q is not None:
                    q_high(q, 0)
                exponentials(a, 0, 1, first)
                if q is not None:
                    q_middle(q, 0)
                    q_high(q, 1)
                attend(a, 0, first, a, 1, q)
                if q is not None:
                    v_text(q, 0)
                    v_text(q, 1)
                heads_out(2 * a.i + 1, 1)
                exponentials(a, 1, 0, False)
                if q is not None:
                    v_image(q)
                exponentials(a, 1, 1, False)
                attend(a, 1, False, q, 0)

            act.wait_ge(sm_k, 1)
            small_k = ps_s[0][:, :, :].rearrange("p j t -> p (j t)")
            nc.scalar.activation(ksm[:, 0, :, :, :].rearrange("p c b r -> p (c b r)"), small_k[:, 0:384],
                                 ACT.Copy).then_inc(sm_hi, 1)
            act.wait_ge(sm_parts, 1)
            k_high(pair(0), 0)
            k_middle(pair(0), 0)
            k_high(pair(0), 1)
            k_middle(pair(0), 1)
            q_high(pair(0), 0)
            q_middle(pair(0), 0)
            q_high(pair(0), 1)
            q_middle(pair(0), 1)
            for g in range(2):
                act.wait_ge(sm_v, g + 1)
                nc.scalar.activation(vsm[:, g, :], ps_o[g][0:B * N_SML, 0:C], ACT.Copy).then_inc(sm_vout, 1)
            act.wait_ge(zeros, 1)
            v_text(pair(0), 0)
            v_text(pair(0), 1)
            v_image(pair(0))
            maxima_out(pair(0), 0)
            nc.scalar.activation(wq_h[0][:, 0:2, :], wq_sb[:, 0:2, :], ACT.Copy).then_inc(w_hi, 1)
            nc.scalar.activation(wq_h[0][0:XC[2], 2, :], wq_sb[0:XC[2], 2, :], ACT.Copy).then_inc(w_hi, 1)
            for g in range(2):
                nc.scalar.activation(wv_h[g][0][:, :, :], wv_sb[g][:, :, :], ACT.Copy).then_inc(w_hi, 1)
            step(pair(1), pair(0), first=True)
            with act.Fori(0, (PAIRS - 2) // 2) as j:
                step(Pair(2 + 2 * j, 0, 1 + j), Pair(1 + 2 * j, 1, j))
                step(Pair(3 + 2 * j, 1, 1 + j), Pair(2 + 2 * j, 0, 1 + j))
            step(None, pair(PAIRS - 1))
            heads_out(B, 0)

        @block.vector
        def _(dve):
            def q_low(q, c):
                dve.wait_ge(q_hi, 2 * q.i + 1 + c)
                if not (isinstance(q.i, int) and q.i == 0):
                    dve.wait_ge(q_parts, 2 * q.i)
                if c == 0:
                    nc.vector.tensor_tensor(qr[:, 0:2, :].rearrange("p c t -> p (c t)"), ps_p[0][:, :],
                                            qp[:, 0, 0:2, :].rearrange("p c t -> p (c t)"), ALU.subtract).then_inc(q_rest, 1)
                else:
                    nc.vector.tensor_tensor(qr[0:XC[2], 2, :], ps_p[1][0:XC[2], 0:T2], qp[0:XC[2], 0, 2, :],
                                            ALU.subtract).then_inc(q_rest, 1)

            def k_low(q, c):
                dve.wait_ge(k_hi, 2 * q.i + 1 + c)
                if not (isinstance(q.i, int) and q.i == 0):
                    dve.wait_ge(k_parts, 2 * q.i)
                if c == 0:
                    src = ps_p[0][:, :].rearrange("p (m t) -> p m t", t=S)
                    hi = kp[:, 0, 0:2, :, :].rearrange("p c b t -> p (c b) t")
                    dst = kr[:, 0:2, :, :].rearrange("p c b t -> p (c b) t")
                    nc.vector.tensor_tensor(dst, src[:, :, 0:N_BIG], hi[:, :, 0:N_BIG], ALU.subtract).then_inc(k_rest, 1)
                else:
                    src = ps_p[1][0:XC[2], 0:T2].rearrange("p (m t) -> p m t", t=S)
                    nc.vector.tensor_tensor(kr[0:XC[2], 2, :, :], src[:, :, 0:N_BIG], kp[0:XC[2], 0, 2, :, 0:N_BIG],
                                            ALU.subtract).then_inc(k_rest, 1)

            def maxima(a, b, t, fresh):
                n = 2 * a.i + b
                dve.wait_ge(s_done, NT * n + t + 1)
                if t == 0 and not fresh:
                    dve.wait_ge(m_parts, n)
                src, hs = ps_s[t % 2], slice(t * HT, (t + 1) * HT)
                nc.vector.tensor_reduce(nm[:, hs, 0:1], src[:, :, 0:N_TXT], AX_X, ALU.max, negate=True)
                nc.vector.tensor_reduce(nm[:, hs, 1:2], src[:, :, N_TXT:N_BIG], AX_X, ALU.max, negate=True)

            def maxima_small(t):
                src, hs = ps_s[t % 2], slice(t * HT, (t + 1) * HT)
                nc.vector.tensor_reduce(nm[:, hs, 2:4], src[:, :, N_BIG:S].rearrange("p j (g t) -> p j g t", g=2),
                                        AX_X, ALU.max, negate=True).then_inc(s_max, 1)

            def split_maxima(a, b, link):
                n = 2 * a.i + b
                nm_v = nm[:, :, :].rearrange("p (h f) g -> p f g h", f=2)
                if link == 0:
                    dve.wait_ge(s_max, NT * (n + 1))
                    nc.vector.tensor_copy(mp[:, :, 0, :, :], nm_v).then_inc(m_chain, 1)
                elif link == 1:
                    dve.wait_ge(m_chain, 3 * n + 1)
                    nc.vector.tensor_tensor(nmr[:, :, :, :], nm_v, mp[:, :, 0, :, :], ALU.subtract).then_inc(m_chain, 1)
                elif link == 2:
                    dve.wait_ge(m_chain, 3 * n + 2)
                    nc.vector.tensor_copy(mp[:, :, 1, :, :], nmr[:, :, :, :]).then_inc(m_chain, 1)
                else:
                    dve.wait_ge(m_chain, 3 * n + 3)
                    nc.vector.tensor_tensor(mp[:, :, 2, :, :], nmr[:, :, :, :], mp[:, :, 1, :, :], ALU.subtract).then_inc(m_parts, 1)

            def heads_of(bank):
                return ps_o[bank][:, 0:HT * OW].rearrange("p (j w) -> p j w", w=OW)

            def invert(a, b, t):
                n = 2 * a.i + b
                bank = (n0(b) + t) % 2
                dve.wait_ge(pv_done, NT * n + t + 1)
                nc.vector.reciprocal(rz[:, bank, :, :], heads_of(bank)[:, :, G * HD:G * HD + G]).then_inc(z_inv, 1)

            def normalise(a, b, t, fresh):
                n = 2 * a.i + b
                bank = (n0(b) + t) % 2
                if t == 0 and not fresh and not (first_pair(a) and b == 1):
                    dve.wait_ge(o_sum, n - 1)
                dve.wait_ge(z_inv, NT * n + t + 1)
                nc.vector.tensor_tensor(og[:, b, t * HT:(t + 1) * HT, :, :].rearrange("p j g d -> p (j g) d"),
                                        heads_of(bank)[:, :, 0:G * HD].rearrange("p j (g d) -> p j g d", g=G),
                                        rz[:, bank, :, :].rearrange("p j (g o) -> p j g o", o=1).to_broadcast([128, HT, G, HD]),
                                        ALU.mult).then_inc(o_norm, 1)

            def result(n, b):
                dve.wait_ge(out_done, n)
                dve.wait_ge(xb_done, n)
                flat = ps_t[t_bank(b, NT + 1)][:, :, :].rearrange("p j t -> p (j t)")
                nc.vector.tensor_tensor(res[:, 1 - b, :], flat[:, 0:C], xb[:, 1 - b, :], ALU.add).then_inc(res_done, 1)

            def attend(a, b, fresh, nxt, nb, low=None):
                if nxt is not None:
                    maxima(nxt, nb, 0, False)
                    maxima_small(0)
                for t in range(NT):
                    ahead = nxt is not None and t + 1 < NT
                    if ahead:
                        maxima(nxt, nb, t + 1, False)
                    tail = nxt is not None and t >= NT - 2
                    invert(a, b, t)
                    if ahead:
                        maxima_small(t + 1)
                    if tail:
                        split_maxima(nxt, nb, 2 * (t - NT + 2))
                    normalise(a, b, t, fresh)
                    if tail:
                        split_maxima(nxt, nb, 2 * (t - NT + 2) + 1)
                if low is not None:
                    q_low(low, 1)
                if not fresh:
                    if b == 1 and not first_pair(a):
                        dve.wait_ge(stored[0], 16 * a.i)
                    if b == 0 and not second_pair(a):
                        dve.wait_ge(stored[1], 16 * (a.i - 1))
                    result(2 * a.i + b, b)

            def step(q, a, first=False):
                if q is not None:
                    for c in range(2):
                        k_low(q, c)
                    q_low(q, 0)
                attend(a, 0, first, a, 1, q)
                attend(a, 1, False, q, 0)

            small_k = ps_s[0][:, :, :].rearrange("p j t -> p (j t)")
            nc.vector.memset(small_k, 0.0).then_inc(casts, 1)
            dve.wait_ge(sm_hi, 1)
            nc.vector.tensor_tensor(ksr.rearrange("p c b r -> p (c b r)"), small_k[:, 0:384],
                                    ksm[:, 0, :, :, :].rearrange("p c b r -> p (c b r)"), ALU.subtract).then_inc(sm_rest, 1)
            for c in range(2):
                k_low(pair(0), c)
            for c in range(2):
                q_low(pair(0), c)
            dve.wait_ge(consts, 48)
            nc.vector.tensor_copy(identb[:, :], ident[:, :]).then_inc(casts, 1)
            nc.vector.tensor_copy(krow[:, :], krow_f[:, :]).then_inc(casts, 1)
            for t in range(NT):
                maxima(pair(0), 0, t, True)
                maxima_small(t)
            for link in range(4):
                split_maxima(pair(0), 0, link)
            dve.wait_ge(w_hi, 4)
            nc.vector.tensor_tensor(wq_h[1][:, 0:2, :], wq_sb[:, 0:2, :], wq_h[0][:, 0:2, :].bitcast(F32),
                                    ALU.subtract).then_inc(w_lo, 1)
            nc.vector.tensor_tensor(wq_h[1][0:XC[2], 2, :], wq_sb[0:XC[2], 2, :], wq_h[0][0:XC[2], 2, :].bitcast(F32),
                                    ALU.subtract).then_inc(w_lo, 1)
            for g in range(2):
                nc.vector.tensor_tensor(wv_h[g][1][:, :, :], wv_sb[g][:, :, :], wv_h[g][0][:, :, :].bitcast(F32),
                                        ALU.subtract).then_inc(w_lo, 1)
            step(pair(1), pair(0), first=True)
            step(pair(2), pair(1))
            step(pair(3), pair(2))
            with dve.Fori(0, (PAIRS - 4) // 2) as j:
                step(Pair(4 + 2 * j, 0, 2 + j), Pair(3 + 2 * j, 1, 1 + j))
                step(Pair(5 + 2 * j, 1, 2 + j), Pair(4 + 2 * j, 0, 2 + j))
            step(None, pair(PAIRS - 1))
            dve.wait_ge(stored[1], 16 * (PAIRS - 1))
            result(B, 0)

        @block.gpsimd
        def _(pool):
            def sum_groups(n, b):
                pool.wait_ge(o_norm, NT * (n + 1))
                g_v = og[:, b, :, :, :].rearrange("p h (x y) d -> p h x (y d)", x=2)
                s_v = os[:, :, :, :].rearrange("p h y d -> p h (y d)")
                nc.gpsimd.tensor_tensor(s_v, g_v[:, :, 0, :], g_v[:, :, 1, :], ALU.add).then_inc(o_half, 1)
                pool.wait_ge(o_half, n + 1)
                nc.gpsimd.tensor_tensor(on[:, b, :].rearrange("p (h d) -> p h d", d=HD), os[:, :, 0, :], os[:, :, 1, :],
                                        ALU.add).then_inc(o_sum, 1)

            def add_bias(a, b):
                pool.wait_ge(xn_in[b], 16 * (a + 1))
                nc.gpsimd.tensor_tensor(xb[:, b, :], xn_sb[:, b, :], bias[:, :], ALU.add).then_inc(xb_done, 1)

            def q_split(q, c):
                rows, cs = (128, slice(0, 2)) if c == 0 else (XC[2], slice(2, 3))
                pool.wait_ge(q_mid, 2 * q.i + 1 + c)
                nc.gpsimd.tensor_tensor(qp[0:rows, 2, cs, :], qr[0:rows, cs, :], qp[0:rows, 1, cs, :],
                                        ALU.subtract).then_inc(q_parts, 1)

            def k_split(q):
                for c in range(2):
                    rows, cs = (128, slice(0, 2)) if c == 0 else (XC[2], slice(2, 3))
                    def view(x):
                        return x.rearrange("p c b t -> p (c b) t")
                    rest = view(kr[0:rows, cs, :, :])
                    mid = view(kp[0:rows, 1, cs, :, 0:N_BIG])
                    pool.wait_ge(k_mid, 2 * q.i + 1 + c)
                    nc.gpsimd.tensor_tensor(view(kp[0:rows, 2, cs, :, 0:N_BIG]), rest, mid, ALU.subtract).then_inc(k_parts, 1)

            def low_halves(q):
                for c in range(2):
                    rows, cs = (128, slice(0, 2)) if c == 0 else (XC[2], slice(2, 3))
                    pool.wait_ge(x_hi, 2 * q.i - 1 + c)
                    nc.gpsimd.tensor_tensor(xT_h[1][0:rows, cs, :], xT_sb[0:rows, q.par, cs, :],
                                            xT_h[0][0:rows, cs, :].bitcast(F32), ALU.subtract).then_inc(x_lo, 1)

            def low_context(q):
                pool.wait_ge(c_hi, q.i)
                nc.gpsimd.tensor_tensor(cT_h[1][:, :, :], cT_sb[:, q.par, :, :], cT_h[0][:, :, :].bitcast(F32),
                                        ALU.subtract).then_inc(c_lo, 1)

            def finish(a, b, q=None):
                n = 2 * a.i + b - 1
                if not (first_pair(a) or (second_pair(a) and b == 0)):
                    pool.wait_ge(ot_done, n - 1)
                    pool.wait_ge(res_done, n - 1)
                sum_groups(n, 1 - b)
                if q is not None:
                    q_split(q, 1)
                add_bias(a.i - (1 - b), 1 - b)

            def step(q, a, first=False):
                if not first:
                    finish(a, 0)
                if q is not None:
                    low_halves(q)
                    k_split(q)
                    low_context(q)
                    q_split(q, 0)
                finish(a, 1, q)

            nc.gpsimd.memset(vbd[:, :, :, 0:G, :].rearrange("p q b g n -> p (q b) (g n)"), 0.0).then_inc(zeros, 1)
            pool.wait_ge(sm_rest, 1)
            nc.gpsimd.tensor_copy(ksm[:, 1, :, :, :], ksr).then_inc(sm_mid, 1)
            pool.wait_ge(sm_mid, 1)
            nc.gpsimd.tensor_tensor(ksm[:, 2, :, :, :], ksr, ksm[:, 1, :, :, :], ALU.subtract).then_inc(sm_parts, 1)
            k_split(pair(0))
            for c in range(2):
                q_split(pair(0), c)
            pool.wait_ge(consts, 48)
            pool.wait_ge(sm_dram, 32)
            step(pair(1), pair(0), first=True)
            step(pair(2), pair(1))
            step(pair(3), pair(2))
            with pool.Fori(0, (PAIRS - 4) // 2) as j:
                step(Pair(4 + 2 * j, 0, 2 + j), Pair(3 + 2 * j, 1, 1 + j))
                step(Pair(5 + 2 * j, 1, 2 + j), Pair(4 + 2 * j, 0, 2 + j))
            step(None, pair(PAIRS - 1))
            pool.wait_ge(ot_done, B - 2)
            sum_groups(B - 1, 1)
            pool.wait_ge(res_done, B - 2)
            add_bias(PAIRS - 1, 1)


def t_bank(b, position):
    return (b * (NT + 2) + position) % 2


def n0(b):
    return b * NT


def first_pair(a):
    return isinstance(a.i, int) and a.i == 0


def second_pair(a):
    return isinstance(a.i, int) and a.i == 1


def kernel(**inputs):
    import concourse.bacc as _bacc
    from concourse.bass_utils import run_bass_kernel_spmd as _run

    x = np.asarray(inputs["x"])
    ctx = np.asarray(inputs["ctx_2048"])
    w = {k: np.asarray(v) for k, v in inputs.items() if k.startswith("L0_xattn_")}
    p = "L0_xattn_to_"
    cols = [(2 * h + c) * HD + d for c in range(2) for d in range(HD) for h in range(8)]
    cols += [(16 + h) * HD + d for d in range(HD) for h in range(H - 16)]
    xT = np.ascontiguousarray(x.reshape(PAIRS, T2, C).transpose(0, 2, 1))
    e = [0, N_TXT, N_TXT + N_OBJ, N_TXT + N_OBJ + N_OTH, S]
    grp = [ctx[:, e[g]:e[g + 1], :] for g in range(G)]
    big = [grp[g].reshape(PAIRS, -1, CA) for g in (0, 3)]
    cM = np.ascontiguousarray(np.concatenate(big, axis=1).transpose(0, 2, 1))
    cS = np.ascontiguousarray(np.concatenate([grp[g].reshape(-1, CA) for g in (1, 2)], axis=0).T)
    group_of = np.repeat(np.arange(G), [N_TXT, N_IP, N_OBJ, N_OTH])
    krow = np.zeros((3, G, 2, S), np.float32)
    ind = np.zeros((S, H, HD), np.float32)
    for g in range(G):
        krow[:, g, :, group_of == g] = 1.0
        ind[group_of == g, :, g] = 1.0
    arrays = {
        "xT": xT, "xn": np.ascontiguousarray(x.reshape(B * S, C)), "cM": cM, "cS": cS,
        "wq": np.ascontiguousarray(w[p + "q_w"][:, cols]),
        "wkt": np.ascontiguousarray(w[p + "k_w"][:, cols]), "wvt": w[p + "v_w"],
        "wki": np.ascontiguousarray(w[p + "k_ip_w"][:, cols]), "wvi": w[p + "v_ip_w"],
        "wko": np.ascontiguousarray(w[p + "k_object_w"][:, cols]), "wvo": w[p + "v_object_w"],
        "wkh": np.ascontiguousarray(w[p + "k_others_w"][:, cols]), "wvh": w[p + "v_others_w"],
        "wo": w[p + "out_w"], "bo": w[p + "out_b"],
        "ident": np.eye(128, dtype=np.float32), "krow": krow.reshape(MS, T2), "ind": ind.reshape(S, C),
    }
    nc = _bacc.Bacc("TRN2", target_bir_lowering=False, num_devices=1)
    args = []
    for name, a in arrays.items():
        args.append(nc.dram_tensor("in_" + name, a.shape, F32, kind="ExternalInput").ap())
    out = nc.dram_tensor("out_0", (B * S, C), F32, kind="ExternalOutput").ap()
    build(nc, *args, out)
    r = _run(nc, [{"in_" + k: v for k, v in arrays.items()}], core_ids=[0])
    return r.results[0]["out_0"].reshape(B, S, C)
```

```python
from contextlib import ExitStack

import numpy as np

import concourse.bass as bass
from concourse import mybir

F32 = mybir.dt.float32
F32R = mybir.dt.float32r
BF16 = mybir.dt.bfloat16
ALU = mybir.AluOpType
ACT = mybir.ActivationFunctionType
AX_X = mybir.AxisListType.X

B, S, C, CA = 16, 128, 320, 512
H, HD = 20, 16
G = 4
N_TXT, N_OBJ, N_OTH = 77, 4, 4
N_IP = S - N_TXT - N_OBJ - N_OTH
N_BIG = N_TXT + N_IP
N_SML = N_OBJ
PAIRS = B // 2
T2 = 2 * S
SCALE = 1.0 / float(np.sqrt(HD))
KC = CA // 128
XC = [128, 128, C - 256]
HT = 4
NT = H // HT
SLOTS_Q = [0, 0, 0, 1, 1, 2]
SLOTS_K = [0, 1, 2, 0, 1, 0]
KS = HD * len(SLOTS_Q)
HH = H // 2
MS = 3 * G
MR = MS * HH
TERMS_C = [(128, k, i, j) for k in range(2) for i, j in ((0, 0), (0, 1), (1, 0))] + [(128, 2, 0, 0), (XC[2], 2, 1, 0)]
OW = (G + 1) * HD
CHUNKS_01, CHUNK_2 = 0, 1
Q_ORDER, K_ORDER = (CHUNKS_01, CHUNK_2), (CHUNK_2, CHUNKS_01)
RELAY = 2 * len(SLOTS_Q) * 16
N_VDMA = 4 * 16


class Pair:

    def __init__(self, index, parity, use):
        self.i, self.par, self.use = index, parity, use


def pair(i):
    return Pair(i, i % 2, i // 2)


def build(nc, xT, xn, cM, cS, wq, wkt, wvt, wki, wvi, wko, wvo, wkh, wvh, wo, bo, ident_d, krow_d, ind_d, out):
    ctx = ExitStack()
    with ctx:
        def sb(name, shape, dt=F32):
            return ctx.enter_context(nc.sbuf_tensor(name, shape, dt))

        def ps(name, shape):
            return ctx.enter_context(nc.psum_tensor(name, shape, F32))

        def sem(name):
            return ctx.enter_context(nc.semaphore(name))

        wq_then_on = sb("wq_then_on", [128, 3 * C])
        wo_then_res = sb("wo_then_res", [128, 3 * C])
        wq_sb = wq_then_on[:, :].rearrange("p (k n) -> p k n", k=3)
        wo_sb = wo_then_res[:, :].rearrange("p (k n) -> p k n", k=3)
        wk_sb = [sb(f"wk_sb{g}", [128, KC, C]) for g in range(2)]
        wv_sb = [sb(f"wv_sb{g}", [128, KC, C]) for g in range(2)]
        wks_then_pT = sb("wks_then_pT", [128, 2 * KC * C])
        wvs_then_og = sb("wvs_then_og", [128, 2 * KC * C])
        wks_sb = wks_then_pT[:, :].rearrange("p (g k n) -> p g k n", g=2, k=KC)
        wvs_sb = wvs_then_og[:, :].rearrange("p (g k n) -> p g k n", g=2, k=KC)
        wv_then_xn = wv_sb[0]
        xn_sb = wv_then_xn[:, 0:2, :]
        bias = sb("bias", [128, C])
        ident = sb("ident", [128, 128])
        identb = sb("identb", [128, 128], BF16)
        krow_f = sb("krow_f", [MS, T2])
        krow = sb("krow", [MS, T2], BF16)
        wq_h = [sb(f"wq_h{k}", [128, 3, C], F32R) for k in range(2)]
        wo_h = [sb(f"wo_h{k}", [128, 3, C], F32R) for k in range(2)]
        wv_h = [[sb(f"wv_h{g}{k}", [128, KC, C], F32R) for k in range(2)] for g in range(2)]
        xT_sb = sb("xT_sb", [128, 2, 3, T2])
        cT_sb = sb("cT_sb", [128, 2, KC, 2 * N_BIG])
        xT_h = [sb(f"xT_h{k}", [128, 3 - k, T2], F32R) for k in range(2)]
        cT_h = [sb(f"cT_h{k}", [128, KC, 2 * N_BIG], F32R) for k in range(2)]
        cS_then_xb = sb("cS_then_xb", [128, 2 * C])
        cS_sb = cS_then_xb[:, 0:2 * KC * B * N_SML].rearrange("p (k r) -> p k r", k=KC)
        xb = cS_then_xb[:, :].rearrange("p (b n) -> p b n", b=2)
        qp = sb("qp", [128, 3, 3, T2], BF16)
        kp = sb("kp", [128, 3, 3, 2, S], BF16)
        ksm = sb("ksm", [128, 3, 3, B, 2 * N_SML], BF16)
        qr = sb("qr", [128, 3, T2])
        kr_all = sb("kr", [128, 3 * 2 * N_BIG])
        kr = kr_all[:, :].rearrange("p (c b t) -> p c b t", c=3, b=2)
        ksr = kr_all[:, 0:3 * B * 2 * N_SML].rearrange("p (c b r) -> p c b r", c=3, b=B)
        qst = [sb(f"qst{p}", [KS + MS, H, T2], BF16) for p in range(2)]
        kst = [sb(f"kst{p}", [KS + MS, H, T2], BF16) for p in range(2)]
        vbd = sb("vbd", [128, 2, 2, G + 1, C])
        vip = sb("vip", [2 * N_IP, C])
        vsm_then_os = sb("vsm_then_os", [128, 2 * C])
        vsm = vsm_then_os[:, 0:C]
        vs_dram = nc.dram_tensor("vs_dram", (PAIRS, 2, 2 * N_SML, C), F32, kind="Internal").ap()
        nm = sb("nm", [128, H, G])
        nmr = sb("nmr", [128, 2, G, HH])
        mp = sb("mp", [128, 2, 3, G, HH], BF16)
        mT = sb("mT", [MR, 2, 128], BF16)
        pT = wks_then_pT[:, :].rearrange("p (t j s) -> p t j s", t=NT, j=HT)
        rz = sb("rz", [128, 2, HT, G])
        og = wvs_then_og[:, :].rearrange("p (b h g d) -> p b h g d", b=2, h=H, g=G)
        os = vsm_then_os[:, :].rearrange("p (h y d) -> p h y d", h=H, y=2)
        on = wq_then_on[:, 0:2 * 3 * 128].rearrange("p (b n) -> p b n", b=2)
        oT = [sb(f"oT{k}", [128, 2, 3 - k, 128], F32R) for k in range(2)]
        res = wo_then_res[:, 0:2 * C].rearrange("p (b n) -> p b n", b=2)

        ps_s = [ps(f"ps_s{k}", [128, HT, S]) for k in range(2)]
        ps_t = [ps(f"ps_t{k}", [128, HT, S]) for k in range(2)]
        ps_o = [ps(f"ps_o{k}", [128, 512]) for k in range(2)]
        ps_p = [ps(f"ps_p{k}", [128, 512]) for k in range(2)]

        w_ks, w_vs, w_q, w_k, w_v, w_o = (sem(n) for n in ("w_ks", "w_vs", "w_q", "w_k", "w_v", "w_o"))
        consts, zeros, spread_in, krow_in = sem("consts"), sem("zeros"), sem("spread_in"), sem("krow_in")
        w_hi, w_lo, x_hi, x_lo, c_hi, c_lo = (sem(n) for n in ("w_hi", "w_lo", "x_hi", "x_lo", "c_hi", "c_lo"))
        x_in = [sem(f"x_in{p}") for p in range(2)]
        c_in = [sem(f"c_in{p}") for p in range(2)]
        xn_in = [sem(f"xn_in{b}") for b in range(2)]
        casts, bias_in = sem("casts"), sem("bias_in")
        q_done, k_done, v_done = sem("q_done"), sem("k_done"), sem("v_done")
        q_hi, k_hi, q_rest, k_rest = sem("q_hi"), sem("k_hi"), sem("q_rest"), sem("k_rest")
        q_mid, k_mid, k_small = sem("q_mid"), sem("k_mid"), sem("k_small")
        q_parts, k_parts = sem("q_parts"), sem("k_parts")
        q_st = [sem(f"q_st{p}") for p in range(2)]
        k_st = [sem(f"k_st{p}") for p in range(2)]
        v_put, vip_out = sem("v_put"), sem("vip_out")
        v_in = [sem(f"v_in{p}") for p in range(2)]
        s_done, s_max, m_chain, m_parts = sem("s_done"), sem("s_max"), sem("m_chain"), sem("m_parts")
        mt_done, mt_out, m_st = sem("mt_done"), sem("mt_out"), sem("m_st")
        t_done, t_exp, pv_done = sem("t_done"), sem("t_exp"), sem("pv_done")
        z_inv, o_norm, o_half, o_sum = sem("z_inv"), sem("o_norm"), sem("o_half"), sem("o_sum")
        ot_low, x_low2, o_tail = sem("ot_low"), sem("x_low2"), sem("o_tail")
        ot_done, ot_out, out_done, xb_done, res_done = (
            sem(n) for n in ("ot_done", "ot_out", "out_done", "xb_done", "res_done"))
        stored = [sem(f"stored{b}") for b in range(2)]
        sm_k, sm_v, sm_hi, sm_rest, sm_mid, sm_parts, sm_vout, sm_dram = (
            sem(n) for n in ("sm_k", "sm_v", "sm_hi", "sm_rest", "sm_mid", "sm_parts", "sm_vout", "sm_dram"))

        def last_output(n):
            return ps_s[1][:, :, :].rearrange("p j t -> p (j t)") if n == B else ps_p[1][:, :]

        block = ctx.enter_context(nc.Block())

        @block.sync
        def _(sp):
            xn_v = xn.rearrange("(p b q) n -> p b q n", b=2, q=S)
            out_v = out.rearrange("(p b q) n -> p b q n", b=2, q=S)

            def addresses(i, *tensors):
                if not isinstance(i, int):
                    for t in tensors:
                        sp.snap(i * (t.size() // t.shape[0]) * 4)

            def load_x_turned(i, p):
                sp.dma_start(xT_sb[:, p, :, :], xT[i].rearrange("(k p) t -> p k t", p=128)).then_inc(x_in[p], 16)

            def load_tokens(i, p):
                load_x_turned(i, p)
                sp.dma_start(cT_sb[:, p, :, :], cM[i].rearrange("(k p) t -> p k t", p=128)).then_inc(c_in[p], 16)

            def load_next(q):
                addresses(q.i, xT, cM)
                sp.wait_ge(v_done, 3 * (q.i - 1))
                load_tokens(q.i, q.par)

            def stack(q, parts, slots, to, part_done, done, order, groups=(0, 1)):
                for n in groups:
                    c = order[n]
                    for part in range(3):
                        sp.wait_ge(part_done[part], 2 * q.i + 1 + n)
                        for slot in [k for k in range(len(slots)) if slots[k] == part]:
                            rows = slice(HD * slot, HD * slot + HD)
                            if c == CHUNKS_01:
                                sp.dma_start(to[q.par][rows, 0:16, :], parts[:, part, 0:2, :]).then_inc(done[q.par], 16)
                            else:
                                sp.dma_start(to[q.par][rows, 16:H, :], parts[0:XC[2], part, 2, :]).then_inc(done[q.par], 16)

            kp_v = kp[:, :, :, :, :].rearrange("p a c b t -> p a c (b t)")

            def stack_q(q):
                stack(q, qp, SLOTS_Q, qst, (q_hi, q_mid, q_parts), q_st, Q_ORDER)

            def stack_k(q, groups=(0, 1)):
                sp.wait_ge(k_small, 2 * q.i + 1)
                stack(q, kp_v, SLOTS_K, kst, (k_hi, k_mid, k_parts), k_st, K_ORDER, groups)

            def spread_v(q):
                for g in range(2):
                    k0 = N_BIG + g * N_SML
                    sp.dma_start(vbd[k0:k0 + N_SML, q.par, :, 2 + g, :],
                                 vs_dram[q.i, :, g * N_SML:(g + 1) * N_SML, :].rearrange("b t n -> t b n"))\
                      .then_inc(v_in[q.par], 16)
                sp.wait_ge(vip_out, q.i + 1)
                for b in range(2):
                    sp.dma_start(vbd[N_TXT:N_BIG, q.par, b, 1, :], vip[b * N_IP:(b + 1) * N_IP, :])\
                      .then_inc(v_in[q.par], 16)

            def load_x(a, b):
                sp.dma_start(xn_sb[:, b, :], xn_v[a, b]).then_inc(xn_in[b], 16)

            def store(a, b):
                sp.wait_ge(res_done, 2 * a + b + 1)
                sp.dma_start(out_v[a, b], res[:, b, :]).then_inc(stored[b], 16)

            def step(q, a):
                sp.wait_ge(xb_done, 2 * a - 1)
                load_x(a, 0)
                if q is not None:
                    stack_k(q)
                    stack_q(q)
                store(a - 1, 1)
                sp.wait_ge(xb_done, 2 * a)
                load_x(a, 1)
                if q is not None:
                    if not (isinstance(q.i, int) and q.i < 2):
                        sp.wait_ge(pv_done, 2 * NT * (q.i - 1))
                    spread_v(q)
                store(a, 0)

            load_x_turned(0, 0)
            sp.dma_start(wq_sb[:, :, :], wq.rearrange("(k p) n -> p k n", p=128)).then_inc(w_q, 16)
            sp.dma_start(cS_sb[:, :, :], cS.rearrange("(k p) t -> p k t", p=128)).then_inc(w_ks, 16)
            for g, wk in enumerate((wko, wkh)):
                sp.dma_start(wks_sb[:, g, :, :], wk.rearrange("(k p) n -> p k n", p=128)).then_inc(w_ks, 16)
            sp.dma_start(cT_sb[:, 0, :, :], cM[0].rearrange("(k p) t -> p k t", p=128)).then_inc(c_in[0], 16)
            for g, wk in enumerate((wkt, wki)):
                sp.dma_start(wk_sb[g][:, :, :], wk.rearrange("(k p) n -> p k n", p=128)).then_inc(w_k, 16)
            for g, wv in enumerate((wvo, wvh)):
                sp.dma_start(wvs_sb[:, g, :, :], wv.rearrange("(k p) n -> p k n", p=128)).then_inc(w_vs, 16)
            for g, wv in enumerate((wvt, wvi)):
                sp.dma_start(wv_sb[g][:, :, :], wv.rearrange("(k p) n -> p k n", p=128)).then_inc(w_v, 16)
            stack_q(pair(0))
            stack_k(pair(0))
            sp.dma_start(ident[:, :], ident_d).then_inc(consts, 16)
            sp.dma_start(krow_f[:, :], krow_d).then_inc(consts, 16)
            load_tokens(1, 1)
            sp.dma_start(bias[:, :], bo.partition_broadcast(128)).then_inc(bias_in, 16)
            for p in range(2):
                for b in range(2):
                    sp.dma_start(vbd[:, p, b, G, :], ind_d).then_inc(spread_in, 16)
            sp.dma_start(wo_sb[:, :, :], wo.rearrange("(k p) n -> p k n", p=128)).then_inc(w_o, 16)
            sp.wait_ge(casts, 4)
            for p in range(2):
                sp.dma_start(kst[p][KS:KS + MS, :, :], krow[:, :].rearrange("r (o t) -> r o t", o=1)
                             .to_broadcast([MS, H, T2])).then_inc(krow_in, 16)
            sp.wait_ge(sm_vout, 2)
            for g in range(2):
                sp.dma_start(vs_dram.rearrange("p b r n -> (p b) r n")[:, g * N_SML:(g + 1) * N_SML, :],
                             vsm[g * B * N_SML:(g + 1) * B * N_SML, :]).then_inc(sm_dram, 16)
            stack_k(pair(1), groups=(0,))
            sp.wait_ge(sm_dram, 32)
            sp.wait_ge(zeros, 1)
            spread_v(pair(0))
            stack_k(pair(1), groups=(1,))
            stack_q(pair(1))
            sp.wait_ge(w_lo, 3)
            for b in range(2):
                load_x(0, b)
            load_next(pair(2))
            spread_v(pair(1))
            store(0, 0)
            load_next(pair(3))
            step(pair(2), 1)
            with sp.Fori(0, (PAIRS - 4) // 2) as j:
                load_next(Pair(4 + 2 * j, 0, 2 + j))
                step(Pair(3 + 2 * j, 1, 1 + j), 2 + 2 * j)
                load_next(Pair(5 + 2 * j, 1, 2 + j))
                step(Pair(4 + 2 * j, 0, 2 + j), 3 + 2 * j)
            step(pair(PAIRS - 1), PAIRS - 2)
            step(None, PAIRS - 1)
            store(PAIRS - 1, 1)
            for b in range(2):
                sp.wait_ge(stored[b], 16 * PAIRS)

        @block.tensor
        def _(pe):
            def q_chunk(q, to, c):
                cols = slice(c * 128, c * 128 + XC[c])
                if isinstance(q.i, int) and q.i == 0:
                    terms = [(wq_sb[0:XC[k], k, cols], xT_sb[0:XC[k], q.par, k, :]) for k in range(3)]
                else:
                    terms = [(wq_h[i][0:rows, k, cols], xT_h[j][0:rows, k, :]) for rows, k, i, j in TERMS_C]
                for n, (w, x) in enumerate(terms):
                    mm = nc.tensor.matmul(to, w, x, start=(n == 0), stop=(n == len(terms) - 1))
                return mm

            def project_q01(q):
                if isinstance(q.i, int) and q.i == 0:
                    pe.wait_ge(w_q, 16)
                    pe.wait_ge(x_in[0], 16)
                else:
                    pe.wait_ge(k_rest, 2 * q.i + 1)
                    pe.wait_ge(x_lo, q.i)
                    pe.wait_ge(x_low2, q.i)
                for c in range(2):
                    mm = q_chunk(q, ps_p[0][:, c * T2:(c + 1) * T2], c)
                mm.then_inc(q_done, 1)

            def project_q2(q):
                if not (isinstance(q.i, int) and q.i == 0):
                    pe.wait_ge(k_rest, 2 * q.i + 2)
                q_chunk(q, ps_p[1][0:XC[2], 0:T2], 2).then_inc(q_done, 1)

            def k_chunk(q, bank, at, c):
                w = XC[c]
                view = ps_p[bank][0:w, at:at + T2].rearrange("p (b t) -> p b t", b=2)
                for g, (t0, n) in enumerate(((0, N_TXT), (N_TXT, N_IP))):
                    rhs = cT_sb[:, q.par, :, 2 * t0:2 * (t0 + n)].rearrange("p k (b t) -> p k b t", b=2)
                    for k in range(KC):
                        mm = nc.tensor.matmul(view[:, :, t0:t0 + n], wk_sb[g][:, k, c * 128:c * 128 + w],
                                              rhs[:, k, :, :], start=(k == 0), stop=(k == KC - 1))
                return mm

            def project_k2(q):
                pe.wait_ge(c_in[q.par], 16 * (q.use + 1))
                if isinstance(q.i, int) and q.i == 0:
                    pe.wait_ge(q_rest, 1)
                else:
                    pe.wait_ge(vip_out, q.i)
                k_chunk(q, 0, 0, 2).then_inc(k_done, 1)

            def project_k01(q, c):
                if c == 0:
                    if isinstance(q.i, int) and q.i == 0:
                        pe.wait_ge(q_rest, 2)
                    else:
                        pe.wait_ge(v_put, 2 * q.i)
                    k_chunk(q, 1, 0, 0)
                else:
                    k_chunk(q, 1, T2, 1).then_inc(k_done, 1)

            def project_v(q, n, part=(0, 1)):
                if 0 in part:
                    if n < 2 and isinstance(q.i, int) and q.i == 0:
                        pe.wait_ge(k_rest, 1 + n)
                    elif n < 2:
                        pe.wait_ge(q_rest, 2 * q.i + 1 + n)
                    else:
                        pe.wait_ge(v_put, 2 * q.i + 1)
                    if n == 0 and not (isinstance(q.i, int) and q.i == 0):
                        pe.wait_ge(c_lo, q.i)
                t0, m = [(0, N_TXT), (N_TXT, N_TXT), (2 * N_TXT, 2 * N_IP)][n]
                if isinstance(q.i, int) and q.i == 0:
                    terms = [(cT_sb[:, 0, k, t0:t0 + m], wv_sb[n // 2][:, k, :]) for k in range(KC)]
                else:
                    terms = [(cT_h[i][:, k, t0:t0 + m], wv_h[n // 2][j][:, k, :])
                             for k in range(KC) for i, j in ((0, 0), (0, 1), (1, 0))]
                half = len(terms) // 2
                for i in range(half * part[0], half * (part[-1] + 1)):
                    mm = nc.tensor.matmul(ps_p[n % 2][0:m, 0:C], *terms[i], start=(i == 0), stop=(i == len(terms) - 1))
                if 1 in part:
                    mm.then_inc(v_done, 1)

            def score_tile(a, b, t, fresh):
                n = 2 * a.i + b
                if t >= 2:
                    pe.wait_ge(s_max, NT * n + t - 1)
                elif not fresh:
                    if t == 0:
                        pe.wait_ge(s_max, NT * n)
                    else:
                        pe.wait_ge(mt_out, n)
                for j in range(HT):
                    h = t * HT + j
                    mm = nc.tensor.matmul(ps_s[t % 2][:, j, :], qst[a.par][0:KS, h, b * S:(b + 1) * S],
                                          kst[a.par][0:KS, h, b * S:(b + 1) * S], start=True, stop=True)
                mm.then_inc(s_done, 1)

            def turn_maxima(a, b):
                n = 2 * a.i + b
                pe.wait_ge(m_parts, n + 1)
                for half in range(2):
                    mm = nc.tensor.matmul(ps_s[1][0:MR, half, :], mp[:, half, :, :, :].rearrange("p a g h -> p (a g h)"),
                                          identb[:, :], start=True, stop=True)
                mm.then_inc(mt_done, 1)

            def exp_tile(a, b, t, fresh, last=False):
                n = 2 * a.i + b
                bank = t_bank(b, 1 + t)
                if last and t < 2:
                    pe.wait_ge(t_exp, NT * n + t - 1)
                    if b == 0 and t == 0:
                        pe.wait_ge(res_done, n - 1)
                elif t >= 2:
                    pe.wait_ge(t_exp, NT * n + t - 1)
                elif not fresh:
                    if t == 1:
                        pe.wait_ge(ot_low, n)
                    elif not (first_pair(a) and b == 1):
                        pe.wait_ge(res_done, n - 1)
                if t == 0:
                    pe.wait_ge(m_st, 16 * (n + 1))
                for j in range(HT):
                    h = t * HT + j
                    mm = nc.tensor.matmul(ps_t[bank][:, j, :], kst[a.par][:, h, b * S:(b + 1) * S],
                                          qst[a.par][:, h, b * S:(b + 1) * S], start=True, stop=True)
                mm.then_inc(t_done, 1)

            def value_tile(a, b, t, fresh):
                n = 2 * a.i + b
                bank = (n0(b) + t) % 2
                if not (fresh and t < 2):
                    pe.wait_ge(o_norm, NT * n + t - 1)
                if t == 0:
                    pe.wait_ge(v_put, 2 * a.i + 1 + b)
                    pe.wait_ge(v_in[a.par], N_VDMA * (a.use + 1))
                pe.wait_ge(t_exp, NT * n + t + 1)
                for j in range(HT):
                    h = t * HT + j
                    mm = nc.tensor.matmul(ps_o[bank][:, j * OW:(j + 1) * OW], pT[:, t, j, :],
                                          vbd[:, a.par, b, :, h * HD:(h + 1) * HD], start=True, stop=True)
                mm.then_inc(pv_done, 1)

            def turn_heads(n, b, last=False):
                if last:
                    bank = ps_p[0][:, :]
                    if b == 1:
                        pe.wait_ge(ot_low, n - 1)
                    else:
                        pe.wait_ge(vip_out, PAIRS)
                else:
                    bank = ps_t[t_bank(b, 0)][:, :, :].rearrange("p j t -> p (j t)")
                    pe.wait_ge(t_exp, NT * n)
                pe.wait_ge(o_sum, n)
                for c in range(3):
                    cols = slice(c * 128, (c + 1) * 128)
                    mm = nc.tensor.transpose(bank[:, cols], on[:, 1 - b, cols], ident[:, :])
                mm.then_inc(ot_done, 1)

            def turn_heads_tail(c):
                if c == 0:
                    pe.wait_ge(ot_low, B - 1)
                pe.wait_ge(o_tail, (2, 4, 6)[c])
                cols = slice(c * 128, (c + 1) * 128)
                to = ps_p[0][:, cols] if c < 2 else ps_s[0][:, 0, :]
                mm = nc.tensor.transpose(to, on[:, 1, cols], ident[:, :])
                if c > 0:
                    mm.then_inc(ot_done, 1)

            def output(n, b, last=False):
                if last:
                    bank = last_output(n)
                else:
                    bank = ps_t[t_bank(b, NT + 1)][:, :, :].rearrange("p j t -> p (j t)")
                if not last:
                    pe.wait_ge(t_exp, NT * n + NT - 1)
                elif n == B - 1:
                    pe.wait_ge(res_done, n - 1)
                elif n == B - 2:
                    pe.wait_ge(v_put, 2 * PAIRS)
                pe.wait_ge(ot_low, n)
                for m, (rows, k, i, j) in enumerate(TERMS_C):
                    if last and n == B and k == 2 and TERMS_C[m - 1][1] == 1:
                        pe.wait_ge(ot_low, B + 1)
                    mm = nc.tensor.matmul(bank[:, 0:C], oT[j][0:rows, 1 - b, k, :], wo_h[i][0:rows, k, :],
                                          start=(m == 0), stop=(m == len(TERMS_C) - 1))
                mm.then_inc(out_done, 1)

            def attend(a, b, fresh, nxt, nb):
                n = 2 * a.i + b
                if nxt is not None:
                    if nb == 0:
                        pe.wait_ge(q_st[nxt.par], RELAY * (nxt.use + 1))
                        pe.wait_ge(k_st[nxt.par], RELAY * (nxt.use + 1))
                    score_tile(nxt, nb, 0, False)
                    score_tile(nxt, nb, 1, False)
                for t in range(NT):
                    value_tile(a, b, t, fresh)
                    if t + 2 < NT:
                        exp_tile(a, b, t + 2, fresh)
                        if nxt is not None:
                            score_tile(nxt, nb, t + 2, False)
                if not fresh:
                    output(n, b)
                    turn_maxima(nxt, nb)

            def step(q, a, first=False, last=False):
                if first:
                    for t in range(2, 4):
                        score_tile(a, 0, t, True)
                    project_k2(q)
                    score_tile(a, 0, 4, True)
                    project_k01(q, 0)
                    pe.wait_ge(casts, 4)
                    turn_maxima(a, 0)
                    project_k01(q, 1)
                elif q is not None:
                    project_k2(q)
                    for c in range(2):
                        project_k01(q, c)
                if first:
                    pe.wait_ge(w_lo, 3)
                    project_q01(q)
                    project_q2(q)
                    pe.wait_ge(krow_in, 32)
                    for t in range(2):
                        exp_tile(a, 0, t, True)
                    pe.wait_ge(spread_in, 64)
                    pe.wait_ge(consts, 32)
                else:
                    turn_heads(2 * a.i, 0)
                    exp_tile(a, 0, 0, False)
                    if q is not None:
                        project_q01(q)
                    exp_tile(a, 0, 1, False)
                    if q is not None:
                        project_q2(q)
                attend(a, 0, first, a, 1)
                if q is not None:
                    project_v(q, 0)
                    if first:
                        turn_maxima(a, 1)
                    if not last:
                        project_v(q, 1)
                if not last:
                    turn_heads(2 * a.i + 1, 1)
                project_v(q, 2, part=(0,))
                if last:
                    turn_heads(2 * a.i + 1, 1)
                exp_tile(a, 1, 0, False)
                project_v(q, 2, part=(1,))
                exp_tile(a, 1, 1, False)
                if first:
                    pe.wait_ge(w_lo, 4)
                attend(a, 1, False, q, 0)

            pe.wait_ge(casts, 2)
            for _ in range(9):
                nc.tensor.matmul(ps_t[0][:, :, :], qp[:, 0, 0, 0:128], qp[:, 0, 0:2, :], start=True, stop=True)
            project_q01(pair(0))
            project_q2(pair(0))
            pe.wait_ge(w_ks, 48)
            small_k = ps_s[0][:, :, :].rearrange("p j t -> p (j t)")
            for g in range(2):
                for c in range(3):
                    w = XC[c]
                    view = small_k[0:w, c * 128:(c + 1) * 128].rearrange("p (b r) -> p b r", b=B)
                    rhs = cS_sb[:, :, g * B * N_SML:(g + 1) * B * N_SML].rearrange("p k (b t) -> p k b t", b=B)
                    for k in range(KC):
                        mm = nc.tensor.matmul(view[:, :, g * N_SML:(g + 1) * N_SML],
                                              wks_sb[:, g, k, c * 128:c * 128 + w], rhs[:, k, :, :],
                                              start=(k == 0), stop=(k == KC - 1))
            mm.then_inc(sm_k, 1)
            pe.wait_ge(w_k, 32)
            project_k2(pair(0))
            for c in range(2):
                project_k01(pair(0), c)
            pe.wait_ge(w_vs, 32)
            for k in range(KC):
                for g in range(2):
                    rows = slice(g * B * N_SML, (g + 1) * B * N_SML)
                    mm = nc.tensor.matmul(ps_o[g][rows, 0:C], cS_sb[:, k, rows], wvs_sb[:, g, k, :],
                                          start=(k == 0), stop=(k == KC - 1))
            mm.then_inc(sm_v, 1)
            pe.wait_ge(w_v, 32)
            for n in range(2):
                project_v(pair(0), n)
            pe.wait_ge(q_st[0], RELAY)
            pe.wait_ge(k_st[0], RELAY)
            for t in range(2):
                score_tile(pair(0), 0, t, True)
            project_v(pair(0), 2)
            step(pair(1), pair(0), first=True)
            step(pair(2), pair(1))
            with pe.Fori(0, (PAIRS - 4) // 2) as j:
                step(Pair(3 + 2 * j, 1, 1 + j), Pair(2 + 2 * j, 0, 1 + j))
                step(Pair(4 + 2 * j, 0, 2 + j), Pair(3 + 2 * j, 1, 1 + j))
            step(pair(PAIRS - 1), pair(PAIRS - 2), last=True)
            a, n = pair(PAIRS - 1), B - 2
            score_tile(a, 1, 0, False)
            project_v(a, 1, part=(0,))
            score_tile(a, 1, 1, False)
            project_v(a, 1, part=(1,))
            for t in range(2, NT - 1):
                score_tile(a, 1, t, False)
            turn_heads(n, 0, last=True)
            for t in range(2):
                exp_tile(a, 0, t, False, last=True)
            score_tile(a, 1, NT - 1, False)
            for b in range(2):
                for t in range(NT):
                    value_tile(a, b, t, False)
                    if t == 1 and b == 1:
                        turn_heads(n + 1, 1, last=True)
                    if t == NT - 1 and b == 1:
                        for c in range(2):
                            turn_heads_tail(c)
                    if t + 2 < NT:
                        exp_tile(a, b, t + 2, False)
                    if t == 1 and b == 0:
                        turn_maxima(a, 1)
                if b == 0:
                    for t in range(2):
                        exp_tile(a, 1, t, False, last=True)
                output(n + b, b, last=True)
            turn_heads_tail(2)
            output(B, 0, last=True)

        @block.scalar
        def _(act):
            def q_high(q, c):
                act.wait_ge(q_done, 2 * q.i + 1 + c)
                if c == 0:
                    if not (isinstance(q.i, int) and q.i == 0):
                        act.wait_ge(q_st[1 - q.par], RELAY * (q.use + q.par))
                    nc.scalar.activation(qp[:, 0, 0:2, :].rearrange("p c t -> p (c t)"), ps_p[0][:, :],
                                         ACT.Copy).then_inc(q_hi, 1)
                else:
                    nc.scalar.activation(qp[0:XC[2], 0, 2, :], ps_p[1][0:XC[2], 0:T2], ACT.Copy).then_inc(q_hi, 1)

            def k_small_out(q):
                if not (isinstance(q.i, int) and q.i == 0):
                    act.wait_ge(k_st[1 - q.par], RELAY * (q.use + q.par))
                small = ksm[:, :, :, :, :].rearrange("p a c (i b) r -> p i (a c) b r", b=2)
                nc.scalar.activation(kp[:, :, :, :, N_BIG:S].rearrange("p a c b r -> p (a c) b r"),
                                     small[:, q.i, :, :, :], ACT.Copy).then_inc(k_small, 2)

            def k_high(q, n):
                act.wait_ge(k_done, 2 * q.i + 1 + n)
                if K_ORDER[n] == CHUNKS_01:
                    src = ps_p[1][:, :].rearrange("p (m t) -> p m t", t=S)
                    dst = kp[:, 0, 0:2, :, :].rearrange("p c b t -> p (c b) t")
                    nc.scalar.activation(dst[:, :, 0:N_BIG], src[:, :, 0:N_BIG], ACT.Copy).then_inc(k_hi, 1)
                else:
                    src = ps_p[0][0:XC[2], 0:T2].rearrange("p (m t) -> p m t", t=S)
                    nc.scalar.activation(kp[0:XC[2], 0, 2, :, 0:N_BIG], src[:, :, 0:N_BIG], ACT.Copy).then_inc(k_hi, 1)

            def q_middle(q, c):
                act.wait_ge(q_rest, 2 * q.i + 1 + c)
                rows, cs = (128, slice(0, 2)) if c == 0 else (XC[2], slice(2, 3))
                nc.scalar.activation(qp[0:rows, 1, cs, :], qr[0:rows, cs, :], ACT.Copy).then_inc(q_mid, 1)

            def k_middle(q, n):
                act.wait_ge(k_rest, 2 * q.i + 1 + n)
                rows, cs = (128, slice(0, 2)) if K_ORDER[n] == CHUNKS_01 else (XC[2], slice(2, 3))
                nc.scalar.activation(kp[0:rows, 1, cs, :, 0:N_BIG].rearrange("p c b t -> p (c b) t"),
                                     kr[0:rows, cs, :, :].rearrange("p c b t -> p (c b) t"), ACT.Copy).then_inc(k_mid, 1)

            def v_text(q, b, last=False):
                act.wait_ge(v_done, 3 * q.i + (3 if last else 1 + b))
                nc.scalar.activation(vbd[0:N_TXT, q.par, b, 0, :], ps_p[b][0:N_TXT, 0:C], ACT.Copy).then_inc(v_put, 1)

            def v_image(q, last=False):
                act.wait_ge(v_done, 3 * q.i + (2 if last else 3))
                if not (isinstance(q.i, int) and q.i == 0):
                    act.wait_ge(v_in[1 - q.par], N_VDMA * (q.use + q.par))
                nc.scalar.activation(vip[:, :], ps_p[0][0:2 * N_IP, 0:C], ACT.Copy).then_inc(vip_out, 1)

            def heads_out(n, b, last=False):
                act.wait_ge(ot_done, n)
                flat = ps_p[0][:, :] if last else ps_t[t_bank(b, 0)][:, :, :].rearrange("p j t -> p (j t)")
                dst = oT[0][:, 1 - b, :, :].rearrange("p c t -> p (c t)")
                nc.scalar.activation(dst, flat[:, 0:384], ACT.Copy).then_inc(ot_out, 1)

            def maxima_out(a, b):
                n = 2 * a.i + b
                act.wait_ge(mt_done, n + 1)
                if not (first_pair(a) and b == 0):
                    act.wait_ge(m_st, 16 * n)
                nc.scalar.activation(mT[:, :, :], ps_s[1][0:MR, 0:2, :], ACT.Copy).then_inc(mt_out, 1)
                act.wait_ge(mt_out, n + 1)
                act.dma_start(qst[a.par][KS:KS + MS, :, b * S:(b + 1) * S],
                              mT[:, :, :].rearrange("p f q -> p (f q)")).then_inc(m_st, 16)

            def exponentials(a, b, t, fresh):
                n = 2 * a.i + b
                bank = t_bank(b, 1 + t)
                act.wait_ge(t_done, NT * n + t + 1)
                if not fresh:
                    act.wait_ge(pv_done, NT * (n - 1) + t + 1)
                nc.scalar.activation(pT[:, t, :, :], ps_t[bank][:, :, :], ACT.Exp, scale=SCALE)\
                  .then_inc(t_exp, 1)

            def high_halves(q):
                act.wait_ge(x_in[q.par], 16 * (q.use + 1))
                act.wait_ge(q_done, 2 * q.i)
                nc.scalar.activation(xT_h[0][:, :, :], xT_sb[:, q.par, :, :], ACT.Copy).then_inc(x_hi, 1)

            def high_context(q):
                act.wait_ge(c_in[q.par], 16 * (q.use + 1))
                act.wait_ge(v_done, 3 * q.i)
                nc.scalar.activation(cT_h[0][:, :, :], cT_sb[:, q.par, :, :], ACT.Copy).then_inc(c_hi, 1)

            def attend(a, b, fresh, nxt, nb, middle=None):
                for t in range(2, NT):
                    exponentials(a, b, t, fresh)
                    if t == 3 and middle is not None:
                        q_middle(middle, 1)
                if nxt is not None:
                    maxima_out(nxt, nb)

            def step(q, a, first=False, last=False):
                if q is not None:
                    if not first:
                        high_halves(q)
                        high_context(q)
                    k_small_out(q)
                    k_high(q, 0)
                    k_middle(q, 0)
                    if first:
                        maxima_out(a, 0)
                    k_high(q, 1)
                if not first:
                    heads_out(2 * a.i, 0)
                if q is not None:
                    k_middle(q, 1)
                if not first:
                    exponentials(a, 0, 0, False)
                if q is not None:
                    q_high(q, 0)
                if first:
                    q_high(q, 1)
                    exponentials(a, 0, 0, True)
                    q_middle(q, 0)
                    exponentials(a, 0, 1, True)
                else:
                    exponentials(a, 0, 1, False)
                    q_middle(q, 0)
                    q_high(q, 1)
                attend(a, 0, first, a, 1, q)
                if q is not None:
                    v_text(q, 0)
                    if not last:
                        v_text(q, 1)
                if first:
                    act.wait_ge(w_o, 16)
                    nc.scalar.activation(wo_h[0][:, :, :], wo_sb[:, :, :], ACT.Copy).then_inc(w_hi, 1)
                heads_out(2 * a.i + 1, 1)
                exponentials(a, 1, 0, False)
                if q is not None:
                    v_image(q, last)
                exponentials(a, 1, 1, False)
                attend(a, 1, False, q, 0)

            q_high(pair(0), 0)
            q_middle(pair(0), 0)
            q_high(pair(0), 1)
            q_middle(pair(0), 1)
            nc.scalar.activation(wq_h[0][:, :, :], wq_sb[:, :, :], ACT.Copy).then_inc(w_hi, 1)
            act.wait_ge(sm_k, 1)
            small_k = ps_s[0][:, :, :].rearrange("p j t -> p (j t)")
            nc.scalar.activation(ksm[:, 0, :, :, :].rearrange("p c b r -> p (c b r)"), small_k[:, 0:384],
                                 ACT.Copy).then_inc(sm_hi, 1)
            act.wait_ge(sm_parts, 1)
            k_small_out(pair(0))
            k_high(pair(0), 0)
            k_middle(pair(0), 0)
            k_high(pair(0), 1)
            k_middle(pair(0), 1)
            act.wait_ge(w_v, 32)
            for g in range(2):
                nc.scalar.activation(wv_h[g][0][:, :, :], wv_sb[g][:, :, :], ACT.Copy).then_inc(w_hi, 1)
            for g in range(2):
                rows = slice(g * B * N_SML, (g + 1) * B * N_SML)
                act.wait_ge(sm_v, 1)
                nc.scalar.activation(vsm[rows, :], ps_o[g][rows, 0:C], ACT.Copy).then_inc(sm_vout, 1)
            act.wait_ge(zeros, 1)
            v_text(pair(0), 0)
            v_text(pair(0), 1)
            v_image(pair(0))
            high_halves(pair(1))
            high_context(pair(1))
            step(pair(1), pair(0), first=True)
            step(pair(2), pair(1))
            with act.Fori(0, (PAIRS - 4) // 2) as j:
                step(Pair(3 + 2 * j, 1, 1 + j), Pair(2 + 2 * j, 0, 1 + j))
                step(Pair(4 + 2 * j, 0, 2 + j), Pair(3 + 2 * j, 1, 1 + j))
            step(pair(PAIRS - 1), pair(PAIRS - 2), last=True)
            a = pair(PAIRS - 1)
            v_text(a, 1, last=True)
            heads_out(B - 2, 0, last=True)
            for b in range(2):
                for t in range(NT):
                    if t == 4 and b == 0:
                        maxima_out(a, 1)
                    if t == 3 and b == 1:
                        heads_out(B - 1, 1, last=True)
                    exponentials(a, b, t, False)
            act.wait_ge(ot_done, B)
            nc.scalar.activation(oT[0][:, 1, 0:2, :].rearrange("p c t -> p (c t)"), ps_p[0][:, 0:256],
                                 ACT.Copy).then_inc(ot_out, 1)
            act.wait_ge(ot_done, B + 1)
            nc.scalar.activation(oT[0][:, 1, 2, :], ps_s[0][:, 0, :], ACT.Copy).then_inc(ot_out, 1)

        @block.vector
        def _(dve):
            def q_low(q, c):
                dve.wait_ge(q_hi, 2 * q.i + 1 + c)
                if not (isinstance(q.i, int) and q.i == 0):
                    dve.wait_ge(q_parts, 2 * q.i)
                if c == 0:
                    nc.vector.tensor_tensor(qr[:, 0:2, :].rearrange("p c t -> p (c t)"), ps_p[0][:, :],
                                            qp[:, 0, 0:2, :].rearrange("p c t -> p (c t)"), ALU.subtract).then_inc(q_rest, 1)
                else:
                    nc.vector.tensor_tensor(qr[0:XC[2], 2, :], ps_p[1][0:XC[2], 0:T2], qp[0:XC[2], 0, 2, :],
                                            ALU.subtract).then_inc(q_rest, 1)

            def low_half(full, halves):
                nc.vector.tensor_tensor(halves[1][:, :, :], full[:, :, :], halves[0][:, :, :].bitcast(F32),
                                        ALU.subtract).then_inc(w_lo, 1)

            def k_low(q, n):
                dve.wait_ge(k_hi, 2 * q.i + 1 + n)
                if not (isinstance(q.i, int) and q.i == 0):
                    dve.wait_ge(k_parts, 2 * q.i)
                if K_ORDER[n] == CHUNKS_01:
                    src = ps_p[1][:, :].rearrange("p (m t) -> p m t", t=S)
                    hi = kp[:, 0, 0:2, :, :].rearrange("p c b t -> p (c b) t")
                    dst = kr[:, 0:2, :, :].rearrange("p c b t -> p (c b) t")
                    nc.vector.tensor_tensor(dst, src[:, :, 0:N_BIG], hi[:, :, 0:N_BIG], ALU.subtract).then_inc(k_rest, 1)
                else:
                    src = ps_p[0][0:XC[2], 0:T2].rearrange("p (m t) -> p m t", t=S)
                    nc.vector.tensor_tensor(kr[0:XC[2], 2, :, :], src[:, :, 0:N_BIG], kp[0:XC[2], 0, 2, :, 0:N_BIG],
                                            ALU.subtract).then_inc(k_rest, 1)

            def maxima(a, b, t, fresh):
                n = 2 * a.i + b
                dve.wait_ge(s_done, NT * n + t + 1)
                if t == 0 and not fresh:
                    dve.wait_ge(m_parts, n)
                src, hs = ps_s[t % 2], slice(t * HT, (t + 1) * HT)
                nc.vector.tensor_reduce(nm[:, hs, 0:1], src[:, :, 0:N_TXT], AX_X, ALU.max, negate=True)
                nc.vector.tensor_reduce(nm[:, hs, 1:2], src[:, :, N_TXT:N_BIG], AX_X, ALU.max, negate=True)

            def maxima_small(t):
                src, hs = ps_s[t % 2], slice(t * HT, (t + 1) * HT)
                nc.vector.tensor_reduce(nm[:, hs, 2:4], src[:, :, N_BIG:S].rearrange("p j (g t) -> p j g t", g=2),
                                        AX_X, ALU.max, negate=True).then_inc(s_max, 1)

            def split_maxima(a, b, link):
                n = 2 * a.i + b
                nm_v = nm[:, :, :].rearrange("p (h f) g -> p f g h", f=2)
                if link == 0:
                    dve.wait_ge(s_max, NT * (n + 1))
                    nc.vector.tensor_copy(mp[:, :, 0, :, :], nm_v).then_inc(m_chain, 1)
                elif link == 1:
                    dve.wait_ge(m_chain, 3 * n + 1)
                    nc.vector.tensor_tensor(nmr[:, :, :, :], nm_v, mp[:, :, 0, :, :], ALU.subtract).then_inc(m_chain, 1)
                elif link == 2:
                    dve.wait_ge(m_chain, 3 * n + 2)
                    nc.vector.tensor_copy(mp[:, :, 1, :, :], nmr[:, :, :, :]).then_inc(m_chain, 1)
                else:
                    dve.wait_ge(m_chain, 3 * n + 3)
                    nc.vector.tensor_tensor(mp[:, :, 2, :, :], nmr[:, :, :, :], mp[:, :, 1, :, :], ALU.subtract).then_inc(m_parts, 1)

            def heads_of(bank):
                return ps_o[bank][:, 0:HT * OW].rearrange("p (j w) -> p j w", w=OW)

            def invert(a, b, t):
                n = 2 * a.i + b
                bank = (n0(b) + t) % 2
                dve.wait_ge(pv_done, NT * n + t + 1)
                nc.vector.reciprocal(rz[:, bank, :, :], heads_of(bank)[:, :, G * HD:G * HD + G]).then_inc(z_inv, 1)

            def normalise(a, b, t, fresh):
                n = 2 * a.i + b
                bank = (n0(b) + t) % 2
                if t == 0 and not fresh and not (first_pair(a) and b == 1):
                    dve.wait_ge(o_sum, n - 1)
                dve.wait_ge(z_inv, NT * n + t + 1)
                nc.vector.tensor_tensor(og[:, b, t * HT:(t + 1) * HT, :, :].rearrange("p j g d -> p (j g) d"),
                                        heads_of(bank)[:, :, 0:G * HD].rearrange("p j (g d) -> p j g d", g=G),
                                        rz[:, bank, :, :].rearrange("p j (g o) -> p j g o", o=1).to_broadcast([128, HT, G, HD]),
                                        ALU.mult).then_inc(o_norm, 1)

            def x_low(q):
                low = slice(XC[2], 128)
                dve.wait_ge(x_hi, q.i)
                nc.vector.tensor_tensor(xT_h[0][low, 2, :], xT_sb[low, q.par, 2, :],
                                        xT_h[0][low, 2, :].bitcast(F32), ALU.subtract).then_inc(x_low2, 1)

            def heads_low(n, b, last=False):
                dve.wait_ge(ot_out, n)
                flat = ps_p[0][:, :] if last else ps_t[t_bank(b, 0)][:, :, :].rearrange("p j t -> p (j t)")
                low = slice(XC[2], 128)
                nc.vector.tensor_tensor(oT[1][:, 1 - b, :, :].rearrange("p c t -> p (c t)"), flat[:, 0:256],
                                        oT[0][:, 1 - b, 0:2, :].rearrange("p c t -> p (c t)").bitcast(F32), ALU.subtract)
                nc.vector.tensor_tensor(oT[0][low, 1 - b, 2, :], flat[low, 256:384],
                                        oT[0][low, 1 - b, 2, :].bitcast(F32), ALU.subtract).then_inc(ot_low, 1)

            def sum_tail(t):
                heads = slice(t * HT, (t + 1) * HT)
                if t == 0:
                    dve.wait_ge(ot_done, B - 2)
                dve.wait_ge(o_norm, NT * (B - 1) + t + 1)
                for at in (t * HT,) if t < NT - 1 else (t * HT, H):
                    nc.vector.tensor_reduce(on[:, 1, at * HD:(at + HT) * HD].rearrange("p (h d) -> p h d", d=HD),
                                            og[:, 1, heads, :, :].rearrange("p h g d -> p h d g"), AX_X, ALU.add)\
                      .then_inc(o_tail, 1)

            def result(n, b, last=False):
                dve.wait_ge(out_done, n)
                dve.wait_ge(xb_done, n)
                if last:
                    flat = last_output(n)
                else:
                    flat = ps_t[t_bank(b, NT + 1)][:, :, :].rearrange("p j t -> p (j t)")
                nc.vector.tensor_tensor(res[:, 1 - b, :], flat[:, 0:C], xb[:, 1 - b, :], ALU.add).then_inc(res_done, 1)

            def attend(a, b, fresh, nxt, nb, low=None):
                if nxt is not None:
                    maxima(nxt, nb, 0, False)
                    maxima_small(0)
                for t in range(NT):
                    ahead = nxt is not None and t + 1 < NT
                    if ahead:
                        maxima(nxt, nb, t + 1, False)
                    split = nxt is not None and t == NT - 2
                    invert(a, b, t)
                    if ahead:
                        maxima_small(t + 1)
                    if split:
                        split_maxima(nxt, nb, 0)
                    normalise(a, b, t, fresh)
                    if t == 1 and low is not None:
                        q_low(low, 1)
                    if split:
                        for link in range(1, 4):
                            split_maxima(nxt, nb, link)
                if not fresh:
                    if b == 1 and not first_pair(a):
                        dve.wait_ge(stored[0], 16 * a.i)
                    if b == 0 and not second_pair(a):
                        dve.wait_ge(stored[1], 16 * (a.i - 1))
                    result(2 * a.i + b, b)

            def step(q, a, first=False):
                if q is not None:
                    if first:
                        for t in range(NT):
                            if t == NT - 1:
                                k_low(q, 0)
                            maxima(a, 0, t, True)
                            maxima_small(t)
                        for link in range(4):
                            split_maxima(a, 0, link)
                        x_low(q)
                        k_low(q, 1)
                    else:
                        x_low(q)
                        k_low(q, 0)
                        k_low(q, 1)
                if not first:
                    heads_low(2 * a.i, 0)
                if q is not None:
                    q_low(q, 0)
                attend(a, 0, first, a, 1, q)
                if first:
                    dve.wait_ge(w_hi, 4)
                    low_half(wo_sb, wo_h)
                heads_low(2 * a.i + 1, 1)
                attend(a, 1, False, q, 0)

            small_k = ps_s[0][:, :, :].rearrange("p j t -> p (j t)")
            nc.vector.memset(qp[:, 0, 0:2, :], 0.0).then_inc(casts, 1)
            nc.vector.memset(small_k, 0.0).then_inc(casts, 1)
            for c in range(2):
                q_low(pair(0), c)
            dve.wait_ge(sm_hi, 1)
            nc.vector.tensor_tensor(ksr.rearrange("p c b r -> p (c b r)"), small_k[:, 0:384],
                                    ksm[:, 0, :, :, :].rearrange("p c b r -> p (c b r)"), ALU.subtract).then_inc(sm_rest, 1)
            dve.wait_ge(sm_rest, 1)
            nc.vector.tensor_copy(ksm[:, 1, :, :, :], ksr).then_inc(sm_mid, 1)
            dve.wait_ge(sm_mid, 1)
            nc.vector.tensor_tensor(ksm[:, 2, :, :, :], ksr, ksm[:, 1, :, :, :], ALU.subtract).then_inc(sm_parts, 1)
            for c in range(2):
                k_low(pair(0), c)
            dve.wait_ge(w_hi, 1)
            low_half(wq_sb, wq_h)
            for g in range(2):
                dve.wait_ge(w_hi, 2 + g)
                low_half(wv_sb[g], wv_h[g])
            dve.wait_ge(consts, 32)
            nc.vector.tensor_copy(identb[:, :], ident[:, :]).then_inc(casts, 1)
            nc.vector.tensor_copy(krow[:, :], krow_f[:, :]).then_inc(casts, 1)
            step(pair(1), pair(0), first=True)
            step(pair(2), pair(1))
            step(pair(3), pair(2))
            with dve.Fori(0, (PAIRS - 4) // 2) as j:
                step(Pair(4 + 2 * j, 0, 2 + j), Pair(3 + 2 * j, 1, 1 + j))
                step(Pair(5 + 2 * j, 1, 2 + j), Pair(4 + 2 * j, 0, 2 + j))
            a = pair(PAIRS - 1)
            for t in range(NT):
                maxima(a, 1, t, False)
                maxima_small(t)
            heads_low(B - 2, 0, last=True)
            for b in range(2):
                for t in range(NT):
                    if t == 0 and b == 0:
                        split_maxima(a, 1, 0)
                        split_maxima(a, 1, 1)
                    invert(a, b, t)
                    if t == 0 and b == 0:
                        split_maxima(a, 1, 2)
                    normalise(a, b, t, False)
                    if t == 0 and b == 0:
                        split_maxima(a, 1, 3)
                    if b == 1:
                        sum_tail(t)
                    if t == 1 and b == 1:
                        heads_low(B - 1, 1, last=True)
                if b == 0:
                    dve.wait_ge(stored[1], 16 * (PAIRS - 2))
                    result(B - 2, 0, last=True)
            dve.wait_ge(ot_out, B)
            nc.vector.tensor_tensor(oT[1][:, 1, :, :].rearrange("p c t -> p (c t)"), ps_p[0][:, 0:256],
                                    oT[0][:, 1, 0:2, :].rearrange("p c t -> p (c t)").bitcast(F32),
                                    ALU.subtract).then_inc(ot_low, 1)
            dve.wait_ge(ot_out, B + 1)
            nc.vector.tensor_tensor(oT[0][XC[2]:128, 1, 2, :], ps_s[0][XC[2]:128, 0, :],
                                    oT[0][XC[2]:128, 1, 2, :].bitcast(F32), ALU.subtract).then_inc(ot_low, 1)
            for b in range(2):
                dve.wait_ge(stored[b], 16 * (PAIRS - 1))
                result(B - 1 + b, 1 - b, last=True)

        @block.gpsimd
        def _(pool):
            def sum_groups(n, b):
                pool.wait_ge(o_norm, NT * (n + 1))
                g_v = og[:, b, :, :, :].rearrange("p h (x y) d -> p h x (y d)", x=2)
                s_v = os[:, :, :, :].rearrange("p h y d -> p h (y d)")
                nc.gpsimd.tensor_tensor(s_v, g_v[:, :, 0, :], g_v[:, :, 1, :], ALU.add).then_inc(o_half, 1)
                pool.wait_ge(o_half, n + 1)
                nc.gpsimd.tensor_tensor(on[:, b, 0:C].rearrange("p (h d) -> p h d", d=HD), os[:, :, 0, :], os[:, :, 1, :],
                                        ALU.add)
                nc.gpsimd.tensor_tensor(on[:, b, C:384].rearrange("p (h d) -> p h d", d=HD), os[:, 16:H, 0, :],
                                        os[:, 16:H, 1, :], ALU.add).then_inc(o_sum, 1)

            def add_bias(a, b):
                pool.wait_ge(xn_in[b], 16 * (a + 1))
                nc.gpsimd.tensor_tensor(xb[:, b, :], xn_sb[:, b, :], bias[:, :], ALU.add).then_inc(xb_done, 1)

            def q_split(q, c):
                rows, cs = (128, slice(0, 2)) if c == 0 else (XC[2], slice(2, 3))
                pool.wait_ge(q_mid, 2 * q.i + 1 + c)
                nc.gpsimd.tensor_tensor(qp[0:rows, 2, cs, :], qr[0:rows, cs, :], qp[0:rows, 1, cs, :],
                                        ALU.subtract).then_inc(q_parts, 1)

            def k_split(q):
                for n in range(2):
                    rows, cs = (128, slice(0, 2)) if K_ORDER[n] == CHUNKS_01 else (XC[2], slice(2, 3))
                    def view(x):
                        return x.rearrange("p c b t -> p (c b) t")
                    rest = view(kr[0:rows, cs, :, :])
                    mid = view(kp[0:rows, 1, cs, :, 0:N_BIG])
                    pool.wait_ge(k_mid, 2 * q.i + 1 + n)
                    nc.gpsimd.tensor_tensor(view(kp[0:rows, 2, cs, :, 0:N_BIG]), rest, mid, ALU.subtract).then_inc(k_parts, 1)

            def low_halves(q):
                pool.wait_ge(x_hi, q.i)
                nc.gpsimd.tensor_tensor(xT_h[1][:, :, :], xT_sb[:, q.par, 0:2, :],
                                        xT_h[0][:, 0:2, :].bitcast(F32), ALU.subtract).then_inc(x_lo, 1)

            def low_context(q):
                pool.wait_ge(c_hi, q.i)
                nc.gpsimd.tensor_tensor(cT_h[1][:, :, :], cT_sb[:, q.par, :, :], cT_h[0][:, :, :].bitcast(F32),
                                        ALU.subtract).then_inc(c_lo, 1)

            def finish(a, b):
                n = 2 * a.i + b - 1
                if not (first_pair(a) or (second_pair(a) and b == 0)):
                    pool.wait_ge(ot_done, n - 1)
                    pool.wait_ge(res_done, n - 1)
                sum_groups(n, 1 - b)
                add_bias(a.i - (1 - b), 1 - b)

            def step(q, a, first=False):
                if not first:
                    finish(a, 0)
                if q is not None:
                    low_halves(q)
                    k_split(q)
                    low_context(q)
                    q_split(q, 0)
                    q_split(q, 1)
                if first:
                    pool.wait_ge(bias_in, 16)
                    pool.wait_ge(sm_dram, 32)
                finish(a, 1)

            nc.gpsimd.memset(vbd[:, :, :, 0:G, :].rearrange("p q b g n -> p (q b) (g n)"), 0.0).then_inc(zeros, 1)
            for c in range(2):
                q_split(pair(0), c)
            k_split(pair(0))
            step(pair(1), pair(0), first=True)
            step(pair(2), pair(1))
            step(pair(3), pair(2))
            with pool.Fori(0, (PAIRS - 4) // 2) as j:
                step(Pair(4 + 2 * j, 0, 2 + j), Pair(3 + 2 * j, 1, 1 + j))
                step(Pair(5 + 2 * j, 1, 2 + j), Pair(4 + 2 * j, 0, 2 + j))
            step(None, pair(PAIRS - 1))
            pool.wait_ge(res_done, B - 2)
            add_bias(PAIRS - 1, 1)


def t_bank(b, position):
    return (b * (NT + 2) + position) % 2


def n0(b):
    return b * NT


def first_pair(a):
    return isinstance(a.i, int) and a.i == 0


def second_pair(a):
    return isinstance(a.i, int) and a.i == 1


def kernel(**inputs):
    import concourse.bacc as _bacc
    from concourse.bass_utils import run_bass_kernel_spmd as _run

    x = np.asarray(inputs["x"])
    ctx = np.asarray(inputs["ctx_2048"])
    w = {k: np.asarray(v) for k, v in inputs.items() if k.startswith("L0_xattn_")}
    p = "L0_xattn_to_"
    cols = [(2 * h + c) * HD + d for c in range(2) for d in range(HD) for h in range(8)]
    cols += [(16 + h) * HD + d for d in range(HD) for h in range(H - 16)]
    def twice(a):
        return np.ascontiguousarray(np.concatenate([a, a[..., 256:C, :]], axis=-2))

    xT = twice(x.reshape(PAIRS, T2, C).transpose(0, 2, 1))
    e = [0, N_TXT, N_TXT + N_OBJ, N_TXT + N_OBJ + N_OTH, S]
    grp = [ctx[:, e[g]:e[g + 1], :] for g in range(G)]
    big = [grp[g].reshape(PAIRS, -1, CA) for g in (0, 3)]
    cM = np.ascontiguousarray(np.concatenate(big, axis=1).transpose(0, 2, 1))
    cS = np.ascontiguousarray(np.concatenate([grp[g].reshape(-1, CA) for g in (1, 2)], axis=0).T)
    group_of = np.repeat(np.arange(G), [N_TXT, N_IP, N_OBJ, N_OTH])
    krow = np.zeros((3, G, 2, S), np.float32)
    ind = np.zeros((S, H, HD), np.float32)
    for g in range(G):
        krow[:, g, :, group_of == g] = 1.0
        ind[group_of == g, :, g] = 1.0
    arrays = {
        "xT": xT, "xn": np.ascontiguousarray(x.reshape(B * S, C)), "cM": cM, "cS": cS,
        "wq": twice(w[p + "q_w"][:, cols]),
        "wkt": np.ascontiguousarray(w[p + "k_w"][:, cols]), "wvt": w[p + "v_w"],
        "wki": np.ascontiguousarray(w[p + "k_ip_w"][:, cols]), "wvi": w[p + "v_ip_w"],
        "wko": np.ascontiguousarray(w[p + "k_object_w"][:, cols]), "wvo": w[p + "v_object_w"],
        "wkh": np.ascontiguousarray(w[p + "k_others_w"][:, cols]), "wvh": w[p + "v_others_w"],
        "wo": twice(w[p + "out_w"]), "bo": w[p + "out_b"],
        "ident": np.eye(128, dtype=np.float32), "krow": krow.reshape(MS, T2), "ind": ind.reshape(S, C),
    }
    nc = _bacc.Bacc("TRN2", target_bir_lowering=False, num_devices=1)
    args = []
    for name, a in arrays.items():
        args.append(nc.dram_tensor("in_" + name, a.shape, F32, kind="ExternalInput").ap())
    out = nc.dram_tensor("out_0", (B * S, C), F32, kind="ExternalOutput").ap()
    build(nc, *args, out)
    r = _run(nc, [{"in_" + k: v for k, v in arrays.items()}], core_ids=[0])
    return r.results[0]["out_0"].reshape(B, S, C)
```
